# Optimizing a Trainium2 kernel written in Bass

```python
import numpy as np
import jax
import jax.numpy as jnp

def _softmax(x, axis=-1):
    return jax.nn.softmax(x, axis=axis)

def _gelu(x):
    return jax.nn.gelu(x, approximate=True)

def _silu(x):
    return jax.nn.silu(x)

def _sigmoid(x):
    return jax.nn.sigmoid(x)

def _layernorm(x, axis=-1, eps=1e-05):
    m = jnp.mean(x, axis=axis, keepdims=True)
    v = jnp.var(x, axis=axis, keepdims=True)
    return (x - m) / jnp.sqrt(v + eps)

def _scatter_add(tgt, idx, src, axis=0):
    return tgt.at[idx].add(src)

def _segment_sum(src, seg, n):
    return jax.ops.segment_sum(src, seg, n)
kernel_name = 'mk_seq_preln_d1_jaxref_r8_a1c7d1'

def setup_inputs(seed: int=0):
    np.random.seed(seed)
    _w = jnp.asarray

    def _L0_attn_setup():
        import jax, jax.numpy as jnp
        import numpy as np
        B, T, D, C = (8, 256, 128, 128)
        key = jax.random.key(seed)
        ks = jax.random.split(key, 16)
        s = 1.0 / np.sqrt(D)
        so = 1.0 / np.sqrt(C)
        return {'x': jax.random.normal(ks[0], (B, T, D), jnp.float32), 'Wq': jax.random.normal(ks[1], (D, C), jnp.float32) * s, 'bq': jax.random.normal(ks[2], (C,), jnp.float32) * 0.01, 'Wk': jax.random.normal(ks[3], (D, C), jnp.float32) * s, 'bk': jax.random.normal(ks[4], (C,), jnp.float32) * 0.01, 'Wv': jax.random.normal(ks[5], (D, C), jnp.float32) * s, 'bv': jax.random.normal(ks[6], (C,), jnp.float32) * 0.01, 'Wa': jax.random.normal(ks[7], (D, 1), jnp.float32) * s, 'ba': jax.random.normal(ks[8], (1,), jnp.float32) * 0.01, 'Wb': jax.random.normal(ks[9], (D, 1), jnp.float32) * s, 'bb': jax.random.normal(ks[10], (1,), jnp.float32) * 0.01, 'Wg': jax.random.normal(ks[11], (D, C), jnp.float32) * s, 'bg': jax.random.normal(ks[12], (C,), jnp.float32) * 0.01, 'Wo': jax.random.normal(ks[13], (C, D), jnp.float32) * so, 'bo': jax.random.normal(ks[14], (D,), jnp.float32) * 0.01}
    _L0_attn_in = _L0_attn_setup()

    def _L0_ffn_setup():
        import math
        import jax, jax.numpy as jnp
        import numpy as np
        D_MODEL = 128
        D_HIDDEN = 256
        N_EXPERTS = 8
        TOP_K = 2
        CAPACITY_FACTOR = 1.25

        def _moe_forward(x, w_router, w_gate, w_down):
            B, T, D = x.shape
            N = B * T
            xf = x.reshape(N, D)
            logits = xf.astype(jnp.float32) @ w_router.T
            gates = jax.nn.softmax(logits, axis=-1)
            topk_gates, topk_idx = jax.lax.top_k(gates, TOP_K)
            expert_mask = jax.nn.one_hot(topk_idx, N_EXPERTS, dtype=jnp.int32).sum(axis=1)
            capacity = math.ceil(N / N_EXPERTS * CAPACITY_FACTOR)
            position_in_expert = jnp.cumsum(expert_mask, axis=0) - 1
            expert_mask = expert_mask * (position_in_expert < capacity)
            keep = jnp.take_along_axis(expert_mask, topk_idx, axis=1) > 0
            topk_gates = topk_gates * keep
            topk_gates = topk_gates / (topk_gates.sum(axis=-1, keepdims=True) + 1e-06)
            hidden = jax.nn.silu(xf @ w_gate.T)
            combine = (topk_gates[:, :, None] * jax.nn.one_hot(topk_idx, N_EXPERTS, dtype=topk_gates.dtype)).sum(axis=1)
            y = jnp.zeros((N, D), dtype=x.dtype)
            for e in range(N_EXPERTS):
                y = y + combine[:, e:e + 1] * (hidden @ w_down[e].T)
            return y.reshape(B, T, D)
        key = jax.random.key(seed)
        k0, k1, k2, k3 = jax.random.split(key, 4)
        B, T = (2, 256)
        x = jax.random.normal(k0, (B, T, D_MODEL), dtype=jnp.float32)
        w_router = jax.random.normal(k1, (N_EXPERTS, D_MODEL), dtype=jnp.float32) * 0.02
        w_gate = jax.random.normal(k2, (D_HIDDEN, D_MODEL), dtype=jnp.float32) * 0.02
        w_down = jax.random.normal(k3, (N_EXPERTS, D_MODEL, D_HIDDEN), dtype=jnp.float32) * 0.02
        return {'x': x, 'w_router': w_router, 'w_gate': w_gate, 'w_down': w_down}
    _L0_ffn_in = _L0_ffn_setup()
    _d = {'L0_attn_x': _L0_attn_in['x'], 'L0_attn_Wq': _L0_attn_in['Wq'], 'L0_attn_bq': _L0_attn_in['bq'], 'L0_attn_Wk': _L0_attn_in['Wk'], 'L0_attn_bk': _L0_attn_in['bk'], 'L0_attn_Wv': _L0_attn_in['Wv'], 'L0_attn_bv': _L0_attn_in['bv'], 'L0_attn_Wa': _L0_attn_in['Wa'], 'L0_attn_ba': _L0_attn_in['ba'], 'L0_attn_Wb': _L0_attn_in['Wb'], 'L0_attn_bb': _L0_attn_in['bb'], 'L0_attn_Wg': _L0_attn_in['Wg'], 'L0_attn_bg': _L0_attn_in['bg'], 'L0_attn_Wo': _L0_attn_in['Wo'], 'L0_attn_bo': _L0_attn_in['bo'], 'L0_ffn_w_router': _L0_ffn_in['w_router'], 'L0_ffn_w_gate': _L0_ffn_in['w_gate'], 'L0_ffn_w_down': _L0_ffn_in['w_down']}
    _x0 = _d['L0_attn_x']
    _d['L0_attn_x'] = jax.random.normal(jax.random.fold_in(jax.random.key(seed), 1), (8, 512, 128), dtype=_x0.dtype)
    del _x0
    return _d

def reference(L0_attn_x, L0_attn_Wq, L0_attn_bq, L0_attn_Wk, L0_attn_bk, L0_attn_Wv, L0_attn_bv, L0_attn_Wa, L0_attn_ba, L0_attn_Wb, L0_attn_bb, L0_attn_Wg, L0_attn_bg, L0_attn_Wo, L0_attn_bo, L0_ffn_w_router, L0_ffn_w_gate, L0_ffn_w_down):

    def _L0_attn_ref(x, Wq, bq, Wk, bk, Wv, bv, Wa, ba, Wb, bb, Wg, bg, Wo, bo):
        import jax, jax.numpy as jnp
        import numpy as np
        B, T, D, C = (8, 256, 128, 128)
        Bn = x.shape[0]
        Cn = Wq.shape[1]
        q = x @ Wq + bq
        k = x @ Wk + bk
        v = x @ Wv + bv
        k = k / jnp.maximum(jnp.linalg.norm(k, axis=-1, keepdims=True), 1e-12)
        alpha = jax.nn.sigmoid(x @ Wa + ba)
        beta = jax.nn.sigmoid(x @ Wb + bb)
        gate = jax.nn.sigmoid(x @ Wg + bg)
        I = jnp.eye(Cn, dtype=x.dtype)

        def step(S, ins):
            q_t, k_t, v_t, a_t, b_t, g_t = ins
            kkT = k_t[:, :, None] * k_t[:, None, :]
            trans = a_t[:, :, None] * (I - b_t[:, :, None] * kkT)
            vkT = v_t[:, :, None] * k_t[:, None, :]
            S = jnp.einsum('bij,bjk->bik', S, trans) + b_t[:, :, None] * vkT
            o = jnp.einsum('bc,bcd->bd', q_t, S) * g_t
            return (S, o)
        tfirst = lambda a: jnp.swapaxes(a, 0, 1)
        S0 = jnp.zeros((Bn, Cn, Cn), x.dtype)
        _, o = jax.lax.scan(step, S0, (tfirst(q), tfirst(k), tfirst(v), tfirst(alpha), tfirst(beta), tfirst(gate)))
        y = jnp.swapaxes(o, 0, 1) @ Wo + bo
        return y

    def _L0_ffn_ref(x, w_router, w_gate, w_down):
        import math
        import jax, jax.numpy as jnp
        import numpy as np
        D_MODEL = 128
        D_HIDDEN = 256
        N_EXPERTS = 8
        TOP_K = 2
        CAPACITY_FACTOR = 1.25

        def _moe_forward(x, w_router, w_gate, w_down):
            B, T, D = x.shape
            N = B * T
            xf = x.reshape(N, D)
            logits = xf.astype(jnp.float32) @ w_router.T
            gates = jax.nn.softmax(logits, axis=-1)
            topk_gates, topk_idx = jax.lax.top_k(gates, TOP_K)
            expert_mask = jax.nn.one_hot(topk_idx, N_EXPERTS, dtype=jnp.int32).sum(axis=1)
            capacity = math.ceil(N / N_EXPERTS * CAPACITY_FACTOR)
            position_in_expert = jnp.cumsum(expert_mask, axis=0) - 1
            expert_mask = expert_mask * (position_in_expert < capacity)
            keep = jnp.take_along_axis(expert_mask, topk_idx, axis=1) > 0
            topk_gates = topk_gates * keep
            topk_gates = topk_gates / (topk_gates.sum(axis=-1, keepdims=True) + 1e-06)
            hidden = jax.nn.silu(xf @ w_gate.T)
            combine = (topk_gates[:, :, None] * jax.nn.one_hot(topk_idx, N_EXPERTS, dtype=topk_gates.dtype)).sum(axis=1)
            y = jnp.zeros((N, D), dtype=x.dtype)
            for e in range(N_EXPERTS):
                y = y + combine[:, e:e + 1] * (hidden @ w_down[e].T)
            return y.reshape(B, T, D)
        return _moe_forward(x, w_router, w_gate, w_down)
    x = L0_attn_x
    x = x + _L0_attn_ref(_layernorm(x, axis=-1), L0_attn_Wq, L0_attn_bq, L0_attn_Wk, L0_attn_bk, L0_attn_Wv, L0_attn_bv, L0_attn_Wa, L0_attn_ba, L0_attn_Wb, L0_attn_bb, L0_attn_Wg, L0_attn_bg, L0_attn_Wo, L0_attn_bo)
    x = x + _L0_ffn_ref(_layernorm(x, axis=-1), L0_ffn_w_router, L0_ffn_w_gate, L0_ffn_w_down)
    return x

_drawn_inputs = setup_inputs


def setup_inputs(seed=0):
    import zlib

    import numpy as np

    out = dict(_drawn_inputs(seed))
    spreads = {}
    factors = {'L0_attn_bq': 8.0,
     'L0_attn_bk': 8.0,
     'L0_attn_bv': 8.0,
     'L0_attn_bg': 21.855,
     'L0_attn_bo': 5.761,
     'L0_ffn_w_router': 3.038,
     'L0_ffn_w_gate': 2.708,
     'L0_ffn_w_down': 2.688}
    for name, (base, spread) in spreads.items():
        noise = np.random.default_rng([zlib.crc32(name.encode()), seed]).standard_normal(out[name].shape)
        drawn = base * np.exp(spread * noise) if base else spread * noise
        out[name] = jnp.asarray(drawn.astype(out[name].dtype))
    for name, factor in factors.items():
        out[name] = (out[name] * factor).astype(out[name].dtype)
    return out
```

```python
from contextlib import ExitStack

import concourse.bass as bass
from concourse import mybir

F32 = mybir.dt.float32
BF16 = mybir.dt.bfloat16
ALU = mybir.AluOpType
ACT = mybir.ActivationFunctionType
AX = mybir.AxisListType

P = 128
LEVELS = (2, 4, 8, 16, 32, 64)


def gated_delta_moe_kernel(nc, ins, consts, out):
    x = ins["L0_attn_x"]
    B, T, D = x.shape
    NC = T // P
    E = ins["L0_ffn_w_router"].shape[0]
    HID = ins["L0_ffn_w_gate"].shape[0]
    KH = HID // P
    CAPACITY = -(-(B * T * 5) // (4 * E))
    KVW = 2 * P + 1
    NL = len(LEVELS)
    assert D == P and T % P == 0 and B % 2 == 0 and E == 8

    with ExitStack() as ctx:
        def sb(name, shape, dt=F32):
            return ctx.enter_context(nc.sbuf_tensor(name, shape, dt))

        def bank(name):
            return ctx.enter_context(nc.psum_tensor(name, [P, 512], F32))

        def sem(name):
            return ctx.enter_context(nc.semaphore(name))

        eye = sb("eye", [P, NC, P])
        up_mask = sb("up_mask", [P, 1 + NL, P])
        low_mask1 = sb("low_mask1", [P, P])
        prio = sb("prio", [P, NC, E])
        prefix = sb("prefix", [P, 2, P])
        prefix16 = sb("prefix16", [P, 2, P], BF16)
        wq = sb("wq", [P, P])
        wg = sb("wg", [P, P])
        wa_col = sb("wa_col", [P, 1])
        wa_rep = sb("wa_rep", [P, P])
        wkvb = sb("wkvb", [P, KVW])
        kvb_bias = sb("kvb_bias", [P, KVW])
        wo = sb("wo", [P, P])
        bo_bc = sb("bo_bc", [P, P])
        bq_col = sb("bq_col", [P, 1])
        bg_col = sb("bg_col", [P, 1])
        ba_col = sb("ba_col", [P, 1])
        w_router = sb("w_router", [P, E])
        w_gate = sb("w_gate", [P, HID])
        w_down = sb("w_down", [P, KH, E, P])
        pad = sb("pad", [P, 4])
        neg_half = sb("neg_half", [P, NC])

        xin = [sb(f"xin{p}", [P, NC, P]) for p in range(2)]
        x_bo = [sb(f"x_bo{p}", [P, NC, P]) for p in range(2)]
        a_st = sb("a_st", [P, NC, 6])
        a_mv = sb("a_mv", [P, NC, 2])
        a_veps = sb("a_veps", [P, NC])
        a_rstd = sb("a_rstd", [P, NC])
        xn = sb("xn", [P, NC, P])
        xnT = sb("xnT", [P, T])
        alpha = sb("alpha", [P, NC, P])
        alpha0 = sb("alpha0", [P, T + 8])
        alpha_first = sb("alpha_first", [P, T])
        decay_row = [sb(f"decay_row{p}", [P, T]) for p in range(2)]
        gam = sb("gam", [P, T])
        gamT = [sb(f"gamT{p}", [P, T]) for p in range(2)]
        kvb = sb("kvb", [P, NC, KVW + 3])
        ksq = sb("ksq", [P, NC, P])
        kss = sb("kss", [P, NC])
        kss_c = sb("kss_c", [P, NC])
        krn = sb("krn", [P, NC])
        beta = sb("beta", [P, NC])
        decay_col = sb("decay_col", [P, NC])
        neg_ba = [sb(f"neg_ba{p}", [P, NC]) for p in range(2)]
        kn = [sb(f"kn{p}", [P, NC, P]) for p in range(2)]
        kg = [sb(f"kg{p}", [P, NC, P]) for p in range(2)]
        bv = [sb(f"bv{p}", [P, NC, P]) for p in range(2)]
        kT = [sb(f"kT{p}", [P, T]) for p in range(2)]
        qT = [sb(f"qT{p}", [P, T]) for p in range(2)]
        qaT = [sb(f"qaT{p}", [P, T]) for p in range(2)]
        gT = [sb(f"gT{p}", [P, T]) for p in range(2)]
        L = sb("L", [P, NC, P])
        L1 = sb("L1", [P, NC, P])
        R = sb("R", [P, NC, P])
        X = sb("X", [P, NC, P])
        Z = sb("Z", [P, NC, P])
        Zf = [sb(f"Zf{p}", [P, NC, P]) for p in range(2)]

        state = [sb(f"state{p}", [P, 2, P]) for p in range(2)]
        rhs = sb("rhs", [P, P])
        w_wT = sb("w_wT", [P, 2, P])
        pT = sb("pT", [P, P])
        og = sb("og", [P, NC, P])
        x1 = [sb(f"x1_{p}", [P, NC, P]) for p in range(2)]
        c_st = sb("c_st", [P, NC, 6])
        c_mv = sb("c_mv", [P, NC, 2])
        c_veps = sb("c_veps", [P, NC])
        c_rstd = sb("c_rstd", [P, NC])
        xn2 = sb("xn2", [P, NC, P])
        xn2T = sb("xn2T", [P, T])
        sig_h = sb("sig_h", [P, KH, T])
        hT = [sb(f"hT{p}", [P, KH, T]) for p in range(2)]
        lg = sb("lg", [P, NC, E])
        top = sb("top", [P, 4, NC])
        rt = [sb(f"rt{n}", [P, NC, E]) for n in range(10)]
        mask16 = sb("mask16", [P, NC, E], BF16)
        before = sb("before", [P, NC + 1, E])
        before16 = sb("before16", [P, NC, E], BF16)
        sums = sb("sums", [P, 4, NC])
        comb = [sb(f"comb{p}", [P, NC, E]) for p in range(2)]

        psA, psR, psX, psZ, psB0, psB1 = [bank(n) for n in ("psA", "psR", "psX", "psZ", "psB0", "psB1")]
        psF = [bank("psF0"), bank("psF1")]

        names = """w_loaded pool_consts act_consts dve_consts
            a_stats a_aggr a_veps_ready a_rstd_ready xn_ready xb_ready
            xnT_ps xnT_ready alpha_ps alpha_ready kv_ps kv_ready kss_ready kssc_ready krn_ready beta_ready
            alpha0_ready gam_ready decay_ready dcol_ready kn_ready kg_ready bv_ready negba_ready
            kT_ps kT_ready q_ps q_ready qa_ready g_ps g_ready kk_ps L_ready lt_ps L1_ready r1_ready
            X_ready Z_ready R_ps R_ready X_ps Z_ps
            rhs_ps rhs_ready w_ps w_ready qw_ps p_ready s_ps s_ready o_ps og_ready
            y_ps x1_ready c_stats c_aggr c_veps_ready c_rstd_ready xn2_ready xn2T_ps xn2T_ready
            log_ps log_ready h_ps sigh_ready h_ready route soft mask_ready cum_ps sig_ready comb_ready
            f_ps f_done f_acc""".split()
        s = {n: sem(n) for n in names}
        S = type("Sems", (), s)
        x_loaded = [sem(f"x_loaded{p}") for p in range(2)]
        y_stored = [sem(f"y_stored{p}") for p in range(2)]

        block = ctx.enter_context(nc.Block())

        def wait(eng, sm, n):
            if not (isinstance(n, int) and n <= 0):
                eng.wait_ge(sm, n)

        def batches(eng, iteration):
            iteration(0, 0, 0, True, False, False)
            iteration(1, 0, 1, True, True, False)
            with eng.Fori(0, (B - 2) // 2) as j:
                iteration(2 * j + 2, j + 1, 0, True, True, True)
                iteration(2 * j + 3, j + 1, 1, True, True, True)
            iteration(B, B // 2, 0, False, True, True)
            iteration(B + 1, B // 2, 1, False, False, True)

        def ch(t, c):
            return t[:, c * P:(c + 1) * P]

        def flat(t):
            return t[:, :, :].rearrange("p c d -> p (c d)")

        N_LOADS = 20

        @block.sync
        def _(sp):
            col = lambda ap: ap.rearrange("(d o) -> d o", o=1)
            loads = [
                (wq[:, :], ins["L0_attn_Wq"]), (wg[:, :], ins["L0_attn_Wg"]), (wa_col[:, :], ins["L0_attn_Wa"]),
                (wkvb[:, 0:P], ins["L0_attn_Wk"]), (wkvb[:, P:2 * P], ins["L0_attn_Wv"]),
                (wkvb[:, 2 * P:KVW], ins["L0_attn_Wb"]),
                (kvb_bias[:, 0:P], ins["L0_attn_bk"].partition_broadcast(P)),
                (kvb_bias[:, P:2 * P], ins["L0_attn_bv"].partition_broadcast(P)),
                (kvb_bias[:, 2 * P:KVW], ins["L0_attn_bb"].partition_broadcast(P)),
                (bq_col[:, :], col(ins["L0_attn_bq"])), (bg_col[:, :], col(ins["L0_attn_bg"])),
                (ba_col[:, :], ins["L0_attn_ba"].partition_broadcast(P)),
                (bo_bc[:, :], ins["L0_attn_bo"].partition_broadcast(P)),
                (eye[:, :, :], consts["eye"]), (up_mask[:, :, :], consts["up_mask"]),
                (low_mask1[:, :], consts["low_mask1"]), (prefix[:, :, :], consts["prefix"]),
                (wo[:, :], ins["L0_attn_Wo"]), (w_router[:, :], ins["w_router_T"]),
                (w_gate[:, :], ins["w_gate_T"]),
            ]
            assert len(loads) == N_LOADS
            sp.dma_start(xin[0][:, :, :], x[0].rearrange("(c p) d -> p c d", p=P)).then_inc(x_loaded[0], 16)
            for dst, src in loads:
                sp.dma_start(dst, src).then_inc(S.w_loaded, 16)
            sp.dma_start(w_down[:, :, :, :], ins["w_down_T"].rearrange("(k p) e d -> p k e d", p=P)).then_inc(S.w_loaded, 16)
            sp.dma_start(prio[:, :, :], consts["prio"]).then_inc(S.w_loaded, 16)

            def iteration(i, h, p, A, Bs, F):
                if A and not (isinstance(i, int) and i == 0):
                    wait(sp, S.xn_ready, NC * (i - 1))
                    sp.dma_start(xin[p][:, :, :], x[i].rearrange("(c p) d -> p c d", p=P)).then_inc(x_loaded[p], 16)
                if F:
                    wait(sp, S.f_acc, NC * E * i)
                    sp.dma_start(out[i - 2].rearrange("(c p) d -> p c d", p=P), x1[p][:, :, :]).then_inc(y_stored[p], 16)

            batches(sp, iteration)
            for p in range(2):
                sp.wait_ge(y_stored[p], 16 * (B // 2 + 1))

        W_ALL = 16 * (N_LOADS + 2)

        @block.gpsimd
        def _(pool):
            pool.memset(neg_half[:, :], -0.5).then_inc(S.pool_consts, 1)
            pool.wait_ge(S.w_loaded, W_ALL)
            pool.wait_ge(S.pool_consts, 1)

            def iteration(i, h, p, A, Bs, F):
                if A:
                    pool.wait_ge(x_loaded[p], 16 * (h + 1))
                    wait(pool, S.x1_ready, i - 1)
                    pool.tensor_tensor(x_bo[p][:, :, :], xin[p][:, :, :],
                                       bo_bc[:, :].unsqueeze(1).to_broadcast([P, NC, P]), ALU.add).then_inc(S.xb_ready, 1)
                    pool.wait_ge(S.a_veps_ready, i + 1)
                    pool.tensor_tensor(a_rstd[:, :], a_veps[:, :], neg_half[:, :], ALU.pow).then_inc(S.a_rstd_ready, 1)
                    pool.wait_ge(S.kssc_ready, i + 1)
                    pool.tensor_tensor(krn[:, :], kss_c[:, :], neg_half[:, :], ALU.pow).then_inc(S.krn_ready, 1)
                    pool.wait_ge(S.L_ready, NC * (i + 1))
                    pool.tensor_tensor(L1[:, :, :], L[:, :, :],
                                       low_mask1[:, :].unsqueeze(1).to_broadcast([P, NC, P]), ALU.mult).then_inc(S.L1_ready, 1)
                    pool.wait_ge(S.L1_ready, i + 1)
                    wait(pool, S.Z_ready, (NL + 1) * i)
                    pool.tensor_tensor(X[:, :, :], eye[:, :, :], L1[:, :, :], ALU.subtract).then_inc(S.X_ready, 1)
                    pool.wait_ge(S.q_ready, i + 1)
                    pool.wait_ge(S.decay_ready, i + 1)
                    wait(pool, S.og_ready, NC * (i - 1))
                    pool.tensor_tensor(qaT[p][:, :], qT[p][:, :], decay_row[p][:, :], ALU.mult).then_inc(S.qa_ready, 1)
                if Bs:
                    pool.wait_ge(S.c_veps_ready, i)
                    pool.tensor_tensor(c_rstd[:, :], c_veps[:, :], neg_half[:, :], ALU.pow).then_inc(S.c_rstd_ready, 1)

            batches(pool, iteration)

        @block.scalar
        def _(act):
            act.wait_ge(S.w_loaded, W_ALL)
            nc.scalar.activation(prefix16[:, :, :], prefix[:, :, :], ACT.Copy).then_inc(S.act_consts, 1)
            nc.scalar.activation(wa_rep[:, :], wa_col[:, :].to_broadcast([P, P]), ACT.Copy).then_inc(S.act_consts, 1)

            def iteration(i, h, p, A, Bs, F):
                q = 1 - p

                def w_copy(c):
                    n = NC * (i - 1) + c
                    act.wait_ge(S.w_ps, n + 1)
                    wait(act, S.og_ready, n)
                    act.activation(w_wT[:, :, :], psB0[:, P:3 * P].rearrange("p (a d) -> p a d", a=2), ACT.Copy).then_inc(S.w_ready, 1)

                if A:
                    act.wait_ge(S.xnT_ps, i + 1)
                    act.activation(xnT[:, :], psA[:, :], ACT.Copy).then_inc(S.xnT_ready, 1)
                    act.wait_ge(S.alpha_ps, i + 1)
                    wait(act, S.dcol_ready, i)
                    act.activation(flat(alpha), psA[:, :], ACT.Sigmoid, bias=ba_col[:, 0:1]).then_inc(S.alpha_ready, 1)
                if Bs:
                    w_copy(0)
                if A:
                    for c in range(NC):
                        act.wait_ge(S.kv_ready, NC * i + c + 1)
                        act.activation(ksq[:, c, :], kvb[:, c, 0:P], ACT.Square, accum_out=kss[:, c:c + 1]).then_inc(S.kss_ready, 1)
                    act.activation(beta[:, :], kvb[:, :, 2 * P], ACT.Sigmoid).then_inc(S.beta_ready, 1)
                if Bs:
                    w_copy(1)
                if A:
                    act.wait_ge(S.kT_ps, i + 1)
                    wait(act, S.s_ready, (NC - 1) * (i - 1))
                    act.activation(kT[p][:, :], psA[:, :], ACT.Copy).then_inc(S.kT_ready, 1)
                    act.wait_ge(S.q_ps, i + 1)
                    act.activation(qT[p][:, :], psA[:, :], ACT.Identity, bias=bq_col[:, 0:1]).then_inc(S.q_ready, 1)
                if Bs:
                    w_copy(2)
                if A:
                    act.wait_ge(S.g_ps, i + 1)
                    act.activation(gT[p][:, :], psA[:, :], ACT.Sigmoid, bias=bg_col[:, 0:1]).then_inc(S.g_ready, 1)
                if Bs:
                    w_copy(3)
                    act.wait_ge(S.xn2T_ps, i)
                    act.activation(xn2T[:, :], psB1[:, :], ACT.Copy).then_inc(S.xn2T_ready, 1)
                    for k in range(KH):
                        act.wait_ge(S.h_ps, KH * (i - 1) + k + 1)
                        wait(act, S.h_ready, KH * (i - 2) + k + 1)
                        act.activation(sig_h[:, k, :], (psB0 if k else psB1)[:, :], ACT.Sigmoid).then_inc(S.sigh_ready, 1)
                    act.wait_ge(S.soft, 2 * (i - 1) + 1)
                    act.activation(rt[6][:, :, :], rt[5][:, :, :], ACT.Sigmoid).then_inc(S.sig_ready, 1)
                    act.activation(rt[7][:, :, :], rt[5][:, :, :], ACT.Sigmoid, scale=-1.0).then_inc(S.sig_ready, 1)

            batches(act, iteration)

        @block.vector
        def _(dve):
            dve.memset(alpha0[:, :], 0.0).then_inc(S.dve_consts, 1)
            dve.memset(alpha_first[:, :], 0.0).then_inc(S.dve_consts, 1)
            dve.memset(before[:, :, :], 0.0).then_inc(S.dve_consts, 1)
            dve.memset(sums[:, 1, :], 0.0).then_inc(S.f_acc, NC * E)
            dve.memset(sums[:, 2, :], 0.0).then_inc(y_stored[0], 16)
            dve.memset(sums[:, 3, :], 0.0).then_inc(y_stored[1], 16)
            dve.wait_ge(S.w_loaded, W_ALL)
            dve.wait_ge(S.dve_consts, 3)

            def iteration(i, h, p, A, Bs, F):
                q = 1 - p

                def a_norm():
                    dve.wait_ge(x_loaded[p], 16 * (h + 1))
                    for c in range(NC):
                        dve.bn_stats(a_st[:, c, :], xin[p][:, c, :]).then_inc(S.a_stats, 1)
                    dve.wait_ge(S.a_stats, NC * (i + 1))
                    dve.memset(pad[:, 0:1], 0.0)
                    for c in range(NC):
                        dve.bn_aggr(a_mv[:, c, :], a_st[:, c, :]).then_inc(S.a_aggr, 1)
                    dve.wait_ge(S.a_aggr, NC * (i + 1))
                    dve.tensor_scalar(a_veps[:, :], a_mv[:, :, 1], 1e-5, None, ALU.add).then_inc(S.a_veps_ready, 1)

                def a_xn():
                    dve.wait_ge(S.xb_ready, i + 1)
                    dve.wait_ge(S.a_rstd_ready, i + 1)
                    for c in range(NC):
                        dve.tensor_scalar(xn[:, c, :], xin[p][:, c, :], a_mv[:, c, 0:1], a_rstd[:, c:c + 1],
                                          ALU.subtract, ALU.mult).then_inc(S.xn_ready, 1)

                def a_kv(c):
                    dve.wait_ge(S.kv_ps, NC * i + c + 1)
                    dve.tensor_tensor(kvb[:, c, 0:KVW], psA[:, 0:KVW], kvb_bias[:, :], ALU.add).then_inc(S.kv_ready, 1)

                def a_decay():
                    dve.wait_ge(S.alpha_ready, i + 1)
                    dve.tensor_copy(alpha0[:, 0:T].rearrange("p (c t) -> p c t", c=NC)[:, :, 1:P],
                                    alpha[:, :, 1:P]).then_inc(S.alpha0_ready, 1)
                    dve.tensor_copy(alpha_first[:, :].rearrange("p (c t) -> p c t", c=NC)[:, :, 0],
                                    alpha[:, :, 0]).then_inc(S.alpha0_ready, 1)
                    dve.wait_ge(S.alpha0_ready, 2 * (i + 1))
                    dve.tensor_tensor_scan(gam[:, ::-1], alpha0[:, 1:T + 1][:, ::-1], flat(eye)[:, ::-1], 0.0,
                                           ALU.mult, ALU.add).then_inc(S.gam_ready, 1)
                    wait(dve, S.og_ready, NC * (i - 1))
                    dve.tensor_tensor_scan(gamT[p][:, :], alpha0[:, 0:T], flat(eye), 0.0,
                                           ALU.mult, ALU.add).then_inc(S.gam_ready, 1)
                    dve.tensor_tensor_scan(decay_row[p][:, :], alpha0[:, 0:T], alpha_first[:, :], 0.0,
                                           ALU.mult, ALU.add).then_inc(S.decay_ready, 1)
                    dve.wait_ge(S.gam_ready, 2 * (i + 1))
                    dve.tensor_tensor(decay_col[:, :], gam[:, :].rearrange("p (c t) -> p c t", c=NC)[:, :, 0],
                                      alpha[:, :, 0], ALU.mult).then_inc(S.dcol_ready, 1)

                def a_keys():
                    dve.wait_ge(S.kss_ready, NC * (i + 1))
                    dve.tensor_scalar(kss_c[:, :], kss[:, :], 1e-24, None, ALU.max).then_inc(S.kssc_ready, 1)
                    dve.wait_ge(S.beta_ready, i + 1)
                    dve.wait_ge(S.dcol_ready, i + 1)
                    dve.scalar_tensor_tensor(neg_ba[p][:, :], decay_col[:, :], -1.0, beta[:, :],
                                             ALU.mult, ALU.mult).then_inc(S.negba_ready, 1)
                    for c in range(NC):
                        dve.tensor_scalar(bv[p][:, c, :], kvb[:, c, P:2 * P], beta[:, c:c + 1], None,
                                          ALU.mult).then_inc(S.bv_ready, 1)
                    dve.wait_ge(S.krn_ready, i + 1)
                    for c in range(NC):
                        dve.tensor_scalar(kn[p][:, c, :], kvb[:, c, 0:P], krn[:, c:c + 1], None,
                                          ALU.mult).then_inc(S.kn_ready, 1)
                    dve.wait_ge(S.kn_ready, NC * (i + 1))
                    for c in range(NC):
                        dve.tensor_scalar(kg[p][:, c, :], kn[p][:, c, :], gamT[p][:, c * P + P - 1:c * P + P], None,
                                          ALU.mult).then_inc(S.kg_ready, 1)

                def a_L():
                    dve.wait_ge(S.kk_ps, i + 1)
                    wait(dve, S.R_ps, NL * i)
                    for c in range(NC):
                        dve.scalar_tensor_tensor(L[:, c, :], psR[:, c * P:(c + 1) * P], beta[:, c:c + 1],
                                                 ch(gam, c), ALU.mult, ALU.mult).then_inc(S.L_ready, 1)

                def a_Z1():
                    dve.wait_ge(S.lt_ps, i + 1)
                    dve.tensor_tensor(R[:, :, :], psX[:, :].rearrange("p (c t) -> p c t", c=NC),
                                      up_mask[:, 0, :].unsqueeze(1).to_broadcast([P, NC, P]), ALU.mult).then_inc(S.r1_ready, 1)
                    dve.wait_ge(S.r1_ready, i + 1)
                    dve.tensor_tensor(Z[:, :, :], eye[:, :, :], R[:, :, :], ALU.subtract).then_inc(S.Z_ready, 1)

                def a_R(l):
                    dve.wait_ge(S.R_ps, NL * i + l + 1)
                    dve.tensor_tensor(R[:, :, :], psR[:, :].rearrange("p (c t) -> p c t", c=NC),
                                      up_mask[:, 1 + l, :].unsqueeze(1).to_broadcast([P, NC, P]), ALU.mult).then_inc(S.R_ready, 1)

                def a_XZ(l):
                    dve.wait_ge(S.Z_ps, NL * i + l + 1)
                    dst = Z
                    if l == NL - 1:
                        dst = Zf[p]
                        wait(dve, S.w_ps, NC * (i - 1))
                    dve.tensor_tensor(flat(dst), flat(Z), psZ[:, :], ALU.subtract).then_inc(S.Z_ready, 1)
                    if l < NL - 1:
                        dve.tensor_tensor(flat(X), flat(X), psX[:, :], ALU.subtract).then_inc(S.X_ready, 1)

                def b_rhs(c):
                    n = NC * (i - 1) + c
                    dve.wait_ge(S.rhs_ps, (NC - 1) * (i - 1) + c)
                    dve.scalar_tensor_tensor(rhs[:, :], psB0[:, 0:P], neg_ba[q][:, c:c + 1], bv[q][:, c, :],
                                             ALU.mult, ALU.add).then_inc(S.rhs_ready, 1)

                def b_p(c):
                    n = NC * (i - 1) + c
                    dve.wait_ge(S.qw_ps, n + 1)
                    dve.tensor_tensor(pT[:, :], psB0[:, 3 * P:4 * P], ch(gamT[q], c), ALU.mult).then_inc(S.p_ready, 1)

                def b_state(c):
                    m = (NC - 1) * (i - 1) + c
                    dve.wait_ge(S.s_ps, m + 1)
                    both = psB1[:, 0:2 * P].rearrange("p (a d) -> p a d", a=2)
                    if c == 0:
                        dve.tensor_copy(state[1][:, :, :], both).then_inc(S.s_ready, 1)
                    else:
                        dve.wait_ge(S.s_ready, m)
                        dve.scalar_tensor_tensor(state[(c + 1) % 2][:, :, :], state[c % 2][:, :, :],
                                                 decay_row[q][:, c * P + P - 1:c * P + P], both,
                                                 ALU.mult, ALU.add).then_inc(S.s_ready, 1)

                def b_o(c):
                    n = NC * (i - 1) + c
                    dve.wait_ge(S.o_ps, n + 1)
                    dve.tensor_tensor(og[:, c, :], psB1[:, 2 * P:3 * P], ch(gT[q], c), ALU.mult).then_inc(S.og_ready, 1)

                def c_norm():
                    dve.wait_ge(S.y_ps, i)
                    dve.wait_ge(S.xb_ready, i)
                    dve.wait_ge(y_stored[q], 16 * (h - q + 1))
                    dve.tensor_tensor(flat(x1[q]), psB0[:, :], flat(x_bo[q]), ALU.add).then_inc(S.x1_ready, 1)
                    dve.wait_ge(S.x1_ready, i)
                    for c in range(NC):
                        dve.bn_stats(c_st[:, c, :], x1[q][:, c, :]).then_inc(S.c_stats, 1)
                    dve.wait_ge(S.c_stats, NC * i)
                    dve.memset(pad[:, 1:2], 0.0)
                    for c in range(NC):
                        dve.bn_aggr(c_mv[:, c, :], c_st[:, c, :]).then_inc(S.c_aggr, 1)
                    dve.wait_ge(S.c_aggr, NC * i)
                    dve.tensor_scalar(c_veps[:, :], c_mv[:, :, 1], 1e-5, None, ALU.add).then_inc(S.c_veps_ready, 1)

                def c_xn():
                    dve.wait_ge(S.c_rstd_ready, i)
                    for c in range(NC):
                        dve.tensor_scalar(xn2[:, c, :], x1[q][:, c, :], c_mv[:, c, 0:1], c_rstd[:, c:c + 1],
                                          ALU.subtract, ALU.mult).then_inc(S.xn2_ready, 1)

                def c_h(k):
                    dve.wait_ge(S.sigh_ready, KH * (i - 1) + k + 1)
                    wait(dve, S.f_acc, NC * E * (i - 1))
                    dve.tensor_tensor(hT[q][:, k, :], (psB0 if k else psB1)[:, :], sig_h[:, k, :],
                                      ALU.mult).then_inc(S.h_ready, 1)

                STEPS = 12

                def bc(t):
                    return t.unsqueeze(2).to_broadcast([P, NC, E])

                def c_top2():
                    def step(k, ins_):
                        ins_.then_inc(S.route, 1)
                        dve.wait_ge(S.route, STEPS * (i - 1) + k)
                    dve.wait_ge(S.log_ps, i)
                    step(1, dve.tensor_copy(lg[:, :, :], psB0[:, 0:NC * E].rearrange("p (c e) -> p c e", c=NC)))
                    step(2, dve.tensor_reduce(top[:, 0, :], lg[:, :, :], AX.X, ALU.max))
                    dve.tensor_tensor(rt[5][:, :, :], lg[:, :, :], bc(top[:, 0, :]), ALU.subtract).then_inc(S.soft, 1)
                    step(3, dve.tensor_tensor(rt[0][:, :, :], lg[:, :, :], bc(top[:, 0, :]), ALU.is_equal))
                    step(4, dve.tensor_tensor(rt[0][:, :, :], rt[0][:, :, :], prio[:, :, :], ALU.mult))
                    step(5, dve.tensor_reduce(top[:, 1, :], rt[0][:, :, :], AX.X, ALU.max))
                    step(6, dve.tensor_tensor(rt[1][:, :, :], prio[:, :, :], bc(top[:, 1, :]), ALU.is_equal))
                    step(7, dve.scalar_tensor_tensor(rt[2][:, :, :], rt[1][:, :, :], -3e38, lg[:, :, :], ALU.mult, ALU.add))
                    step(8, dve.tensor_reduce(top[:, 2, :], rt[2][:, :, :], AX.X, ALU.max))
                    step(9, dve.tensor_tensor(rt[3][:, :, :], rt[2][:, :, :], bc(top[:, 2, :]), ALU.is_equal))
                    step(10, dve.tensor_tensor(rt[3][:, :, :], rt[3][:, :, :], prio[:, :, :], ALU.mult))
                    step(11, dve.tensor_reduce(top[:, 3, :], rt[3][:, :, :], AX.X, ALU.max))
                    step(12, dve.tensor_tensor(rt[4][:, :, :], prio[:, :, :], bc(top[:, 3, :]), ALU.is_equal))
                    dve.tensor_tensor(mask16[:, :, :], rt[4][:, :, :], rt[1][:, :, :], ALU.add).then_inc(S.mask_ready, 1)
                    dve.tensor_tensor(rt[8][:, :, :], rt[4][:, :, :], rt[1][:, :, :], ALU.add).then_inc(S.mask_ready, 1)
                    dve.wait_ge(S.mask_ready, 9 * (i - 1) + 2)
                    for c in range(NC):
                        dve.tensor_tensor(before[:, c + 1, :], before[:, c, :], rt[8][:, c, :], ALU.add).then_inc(S.mask_ready, 1)
                        dve.wait_ge(S.mask_ready, 9 * (i - 1) + 3 + c)
                    dve.tensor_copy(before16[:, :, :], before[:, 0:NC, :]).then_inc(S.mask_ready, 1)
                    dve.wait_ge(S.mask_ready, 9 * (i - 1) + 7)
                    dve.tensor_copy(before[:, 0, :], before[:, NC, :]).then_inc(S.mask_ready, 1)
                    dve.wait_ge(S.mask_ready, 9 * (i - 1) + 8)
                    dve.memset(sums[:, 0, 0:1], 0.0).then_inc(S.mask_ready, 1)

                CS = 9

                def c_comb():
                    def step(k, ins_):
                        ins_.then_inc(S.comb_ready, 1)
                        dve.wait_ge(S.comb_ready, CS * (i - 1) + k)
                    dve.wait_ge(S.sig_ready, 2 * i)
                    step(1, dve.reciprocal(rt[9][:, :, :], rt[7][:, :, :]))
                    step(2, dve.tensor_tensor(rt[6][:, :, :], rt[6][:, :, :], rt[9][:, :, :], ALU.mult))
                    step(3, dve.tensor_reduce(sums[:, 0, :], rt[6][:, :, :], AX.X, ALU.add))
                    step(4, dve.reciprocal(sums[:, 1, :], sums[:, 0, :]))
                    dve.wait_ge(S.cum_ps, i)
                    step(5, dve.scalar_tensor_tensor(rt[2][:, :, :], psB1[:, 0:NC * E].rearrange("p (c e) -> p c e", c=NC),
                                                     float(CAPACITY), rt[8][:, :, :], ALU.is_le, ALU.mult))
                    step(6, dve.tensor_tensor(rt[2][:, :, :], rt[2][:, :, :], rt[6][:, :, :], ALU.mult))
                    step(7, dve.tensor_tensor(rt[2][:, :, :], rt[2][:, :, :], bc(sums[:, 1, :]), ALU.mult))
                    step(8, dve.tensor_reduce(sums[:, 2, :], rt[2][:, :, :], AX.X, ALU.add))
                    dve.tensor_scalar(sums[:, 3, :], sums[:, 2, :], 1e-6, None, ALU.add).then_inc(S.soft, 1)
                    dve.wait_ge(S.soft, 2 * i)
                    dve.reciprocal(top[:, 0, :], sums[:, 3, :]).then_inc(S.log_ready, 1)
                    dve.wait_ge(S.log_ready, i)
                    wait(dve, S.f_acc, NC * E * (i - 1))
                    step(9, dve.tensor_tensor(comb[q][:, :, :], rt[2][:, :, :], bc(top[:, 0, :]), ALU.mult))

                def f_sum(c, h):
                    dve.wait_ge(S.f_ps, 2 * NC * (i - 2) + 2 * c + h + 1)
                    for e in range(4):
                        n = NC * E * (i - 1) + E * c + 4 * h + e
                        if not (c == 0 and h == 0 and e == 0):
                            dve.wait_ge(S.f_acc, n)
                        ins_ = dve.scalar_tensor_tensor(x1[p][:, c, :], psF[h][:, e * P:(e + 1) * P],
                                                        comb[p][:, c, 4 * h + e:4 * h + e + 1], x1[p][:, c, :],
                                                        ALU.mult, ALU.add)
                        ins_.then_inc(S.f_acc, 1)

                if A: a_norm()
                if F: f_sum(0, 0)
                if A: a_xn()
                if Bs: b_state(0); b_p(0)
                if F: f_sum(0, 1)
                if A: a_kv(0); a_kv(1)
                if Bs: b_o(0); b_rhs(1)
                if A: a_kv(2); a_kv(3)
                if F: f_sum(1, 0)
                if A: a_decay()
                if Bs: b_state(1); b_p(1)
                if A: a_keys()
                if Bs: b_o(1); b_rhs(2)
                if F: f_sum(1, 1)
                if A: a_L(); a_Z1()
                if Bs: b_state(2); b_p(2)
                if A: a_R(0)
                if Bs: b_o(2); b_rhs(3)
                if F: f_sum(2, 0)
                if A: a_XZ(0)
                if Bs: b_p(3)
                if A: a_R(1)
                if Bs: b_o(3)
                if F: f_sum(2, 1)
                if A: a_XZ(1)
                if Bs: c_norm()
                if A: a_R(2)
                if F: f_sum(3, 0)
                if Bs: c_xn()
                if A: a_XZ(2)
                if F: f_sum(3, 1)
                if A: a_R(3)
                if Bs: c_h(0)
                if A: a_XZ(3)
                if Bs: c_top2()
                if A: a_R(4)
                if Bs: c_comb()
                if A: a_XZ(4)
                if Bs: c_h(1)
                if A: a_R(5)
                if A: a_XZ(5)

            batches(dve, iteration)

        @block.tensor
        def _(pe):
            pe.wait_ge(S.w_loaded, W_ALL)
            pe.wait_ge(S.act_consts, 2)

            def mm(o, lhsT, r, start=True, stop=True):
                return nc.tensor.matmul(o, lhsT, r, start=start, stop=stop)

            def iteration(i, h, p, A, Bs, F):
                q = 1 - p

                def a_T():
                    wait(pe, S.g_ready, i)
                    for c in range(NC):
                        pe.wait_ge(S.xn_ready, NC * i + c + 1)
                        last = nc.tensor.transpose(psA[:, c * P:(c + 1) * P], xn[:, c, :], eye[:, 0, :])
                    last.then_inc(S.xnT_ps, 1)

                def a_alpha():
                    pe.wait_ge(S.xnT_ready, i + 1)
                    mm(psA[:, :], wa_rep[:, :], xnT[:, :]).then_inc(S.alpha_ps, 1)

                def a_kv(c):
                    if c == 0:
                        pe.wait_ge(S.alpha_ready, i + 1)
                        wait(pe, S.kg_ready, NC * i)
                    else:
                        pe.wait_ge(S.kv_ready, NC * i + c)
                    mm(psA[:, 0:KVW], xnT[:, c * P:(c + 1) * P], wkvb[:, :]).then_inc(S.kv_ps, 1)

                def a_kT():
                    pe.wait_ge(S.kn_ready, NC * (i + 1))
                    for c in range(NC):
                        last = nc.tensor.transpose(psA[:, c * P:(c + 1) * P], kn[p][:, c, :], eye[:, 0, :])
                    last.then_inc(S.kT_ps, 1)

                def a_kk():
                    pe.wait_ge(S.kT_ready, i + 1)
                    wait(pe, S.R_ready, NL * i)
                    for c in range(NC):
                        last = mm(psR[:, c * P:(c + 1) * P], ch(kT[p], c), ch(kT[p], c))
                    last.then_inc(S.kk_ps, 1)

                def a_q():
                    pe.wait_ge(S.kT_ready, i + 1)
                    mm(psA[:, :], wq[:, :], xnT[:, :]).then_inc(S.q_ps, 1)

                def a_g():
                    pe.wait_ge(S.q_ready, i + 1)
                    mm(psA[:, :], wg[:, :], xnT[:, :]).then_inc(S.g_ps, 1)

                def a_LT():
                    pe.wait_ge(S.L_ready, NC * (i + 1))
                    wait(pe, S.X_ready, NL * i)
                    for c in range(NC):
                        last = nc.tensor.transpose(psX[:, c * P:(c + 1) * P], L[:, c, :], eye[:, 0, :])
                    last.then_inc(S.lt_ps, 1)

                def a_R(l):
                    pe.wait_ge(S.Z_ready, (NL + 1) * i + l + 1)
                    for c in range(NC):
                        last = mm(psR[:, c * P:(c + 1) * P], L[:, c, :], Z[:, c, :])
                    last.then_inc(S.R_ps, 1)

                def a_XZ(l):
                    pe.wait_ge(S.R_ready, NL * i + l + 1)
                    pe.wait_ge(S.X_ready, NL * i + l + 1)
                    if l < NL - 1:
                        for c in range(NC):
                            mm(psX[:, c * P:(c + 1) * P], R[:, c, :], X[:, c, :])
                    for c in range(NC):
                        last = mm(psZ[:, c * P:(c + 1) * P], X[:, c, :], R[:, c, :])
                    last.then_inc(S.Z_ps, 1)

                def b_rhs(c):
                    pe.wait_ge(S.s_ready, (NC - 1) * (i - 1) + c)
                    mm(psB0[:, 0:P], ch(kT[q], c), state[c % 2][:, 1, :]).then_inc(S.rhs_ps, 1)

                def b_w(c):
                    if c == 0:
                        pe.wait_ge(S.Z_ready, (NL + 1) * i)
                        pe.wait_ge(S.bv_ready, NC * i)
                        wait(pe, S.h_ready, KH * (i - 1))
                        wait(pe, S.comb_ready, 9 * (i - 1))
                        r = bv[q][:, 0, :]
                    else:
                        pe.wait_ge(S.rhs_ready, (NC - 1) * (i - 1) + c)
                        r = rhs[:, :]
                    mm(psB0[:, P:2 * P], Zf[q][:, c, :], r)
                    mm(psB0[:, 2 * P:3 * P], r, Zf[q][:, c, :]).then_inc(S.w_ps, 1)

                def b_qw_s(c):
                    n = NC * (i - 1) + c
                    pe.wait_ge(S.w_ready, n + 1)
                    if c < NC - 1:
                        pe.wait_ge(S.kg_ready, NC * i)
                        if c:
                            pe.wait_ge(S.og_ready, n)
                        mm(psB1[:, 0:P], w_wT[:, 0, :], kg[q][:, c, :])
                        mm(psB1[:, P:2 * P], kg[q][:, c, :], w_wT[:, 0, :]).then_inc(S.s_ps, 1)
                    pe.wait_ge(S.q_ready, i)
                    mm(psB0[:, 3 * P:4 * P], w_wT[:, 1, :], ch(qT[q], c)).then_inc(S.qw_ps, 1)

                def b_o(c):
                    n = NC * (i - 1) + c
                    if c < NC - 1:
                        pe.wait_ge(S.s_ready, (NC - 1) * (i - 1) + c + 1)
                    else:
                        pe.wait_ge(S.og_ready, n)
                    if c > 0:
                        pe.wait_ge(S.qa_ready, i)
                        mm(psB1[:, 2 * P:3 * P], state[c % 2][:, 0, :], ch(qaT[q], c), stop=False)
                    pe.wait_ge(S.p_ready, n + 1)
                    mm(psB1[:, 2 * P:3 * P], kn[q][:, c, :], pT[:, :], start=c == 0).then_inc(S.o_ps, 1)

                def c_wo():
                    pe.wait_ge(S.og_ready, NC * i)
                    for c in range(NC):
                        last = mm(psB0[:, c * P:(c + 1) * P], og[:, c, :], wo[:, :])
                    last.then_inc(S.y_ps, 1)

                def c_T():
                    pe.wait_ge(S.xn2_ready, NC * i)
                    for c in range(NC):
                        last = nc.tensor.transpose(psB1[:, c * P:(c + 1) * P], xn2[:, c, :], eye[:, 0, :])
                    last.then_inc(S.xn2T_ps, 1)

                def c_logits():
                    pe.wait_ge(S.xn2T_ready, i)
                    for c in range(NC):
                        last = mm(psB0[:, c * E:(c + 1) * E], xn2T[:, c * P:(c + 1) * P], w_router[:, :])
                    last.then_inc(S.log_ps, 1)

                def c_h(k):
                    if k:
                        pe.wait_ge(S.route, 12 * (i - 1) + 1)
                    mm((psB0 if k else psB1)[:, :], w_gate[:, k * P:(k + 1) * P], xn2T[:, :]).then_inc(S.h_ps, 1)

                def c_cum():
                    pe.wait_ge(S.mask_ready, 9 * i)
                    pe.wait_ge(S.h_ready, KH * (i - 1) + 1)
                    m16, b16 = [t[:, :, :].rearrange("p c e -> p (c e)") for t in (mask16, before16)]
                    mm(psB1[:, 0:NC * E], prefix16[:, 0, :], m16, stop=False)
                    mm(psB1[:, 0:NC * E], prefix16[:, 1, :], b16, start=False).then_inc(S.cum_ps, 1)

                def f_mm(c, h):
                    n = 2 * NC * (i - 2) + 2 * c + h
                    if c == 0 and h == 0:
                        pe.wait_ge(S.h_ready, KH * (i - 1))
                    if c == 0:
                        wait(pe, S.f_acc, NC * E * (i - 1) - 4 * (1 - h))
                    else:
                        wait(pe, S.f_acc, NC * E * (i - 1) + E * (c - 1) + 4 * (h + 1))
                    for k in range(KH):
                        last = mm(psF[h][:, :], hT[p][:, k, c * P:(c + 1) * P],
                                  w_down[:, k, 4 * h:4 * h + 4, :].rearrange("p e d -> p (e d)"),
                                  start=k == 0, stop=k == KH - 1)
                    last.then_inc(S.f_ps, 1)

                if F: f_mm(0, 0)
                if A: a_T()
                if A: a_alpha()
                if Bs: b_w(0)
                if F: f_mm(0, 1)
                if Bs: b_qw_s(0)
                if A: a_kv(0); a_kv(1)
                if Bs: b_o(0); b_rhs(1)
                if A: a_kv(2); a_kv(3)
                if F: f_mm(1, 0)
                if Bs: b_w(1); b_qw_s(1)
                if Bs: b_o(1); b_rhs(2)
                if F: f_mm(1, 1)
                if A: a_kT()
                if Bs: b_w(2)
                if A: a_kk(); a_q()
                if A: a_LT()
                if Bs: b_qw_s(2)
                if A: a_R(0)
                if A: a_g()
                if Bs: b_o(2); b_rhs(3)
                if F: f_mm(2, 0)
                if A: a_XZ(0)
                if Bs: b_w(3); b_qw_s(3)
                if A: a_R(1)
                if Bs: b_o(3)
                if F: f_mm(2, 1)
                if A: a_XZ(1)
                if Bs: c_wo()
                if A: a_R(2)
                if F: f_mm(3, 0)
                if A: a_XZ(2)
                if F: f_mm(3, 1)
                if Bs: c_T()
                if A: a_R(3)
                if Bs: c_logits(); c_h(0)
                if A: a_XZ(3)
                if Bs: c_h(1)
                if A: a_R(4)
                if Bs: c_cum()
                if A: a_XZ(4)
                if A: a_R(5)
                if A: a_XZ(5)

            batches(pe, iteration)


_INS = ["L0_attn_x", "L0_attn_Wq", "L0_attn_bq", "L0_attn_Wk", "L0_attn_bk", "L0_attn_Wv", "L0_attn_bv", "L0_attn_Wa",
        "L0_attn_ba", "L0_attn_Wb", "L0_attn_bb", "L0_attn_Wg", "L0_attn_bg", "L0_attn_Wo", "L0_attn_bo",
        "L0_ffn_w_router", "L0_ffn_w_gate", "L0_ffn_w_down"]


def kernel(**inputs):
    import numpy as np
    import concourse.bacc as bacc
    from concourse.bass_utils import run_bass_kernel_spmd

    nc = bacc.Bacc("TRN2", target_bir_lowering=False, num_devices=1)
    arrays = {}

    def dram(name, a):
        a = np.ascontiguousarray(a)
        arrays[f"in_{name}"] = a
        return nc.dram_tensor(f"in_{name}", a.shape, mybir.dt.from_np(a.dtype), kind="ExternalInput").ap()

    ins = {n: dram(n, inputs[n]) for n in _INS}
    ins["w_router_T"] = dram("w_router_T", np.transpose(np.asarray(inputs["L0_ffn_w_router"])))
    ins["w_gate_T"] = dram("w_gate_T", np.transpose(np.asarray(inputs["L0_ffn_w_gate"])))
    ins["w_down_T"] = dram("w_down_T", np.transpose(np.asarray(inputs["L0_ffn_w_down"]), (2, 0, 1)))
    nb, nt, _ = inputs["L0_attn_x"].shape
    chunks, experts = nt // P, inputs["L0_ffn_w_router"].shape[0]
    r, c = np.arange(P)[:, None], np.arange(P)[None, :]
    pair = [(r // m % 2 == 0) & (c // m == r // m + 1) for m in (1,) + LEVELS]
    f = np.float32
    consts = {
        "eye": dram("eye", np.stack([np.eye(P, dtype=f)] * chunks, 1)),
        "up_mask": dram("up_mask", np.stack([m.astype(f) for m in pair], 1)),
        "low_mask1": dram("low_mask1", pair[0].T.astype(f)),
        "prefix": dram("prefix", np.stack([(r <= c).astype(f), np.ones((P, P), f)], 1)),
        "prio": dram("prio", np.broadcast_to(np.arange(experts, 0, -1, dtype=f), (P, chunks, experts))),
    }
    out = nc.dram_tensor("out_y", inputs["L0_attn_x"].shape, F32, kind="ExternalOutput").ap()
    gated_delta_moe_kernel(nc, ins, consts, out)
    return run_bass_kernel_spmd(nc, [arrays], core_ids=[0]).results[0]["out_y"]
```

```python
from contextlib import ExitStack

import concourse.bass as bass
from concourse import mybir

F32 = mybir.dt.float32
BF16 = mybir.dt.bfloat16
ALU = mybir.AluOpType
ACT = mybir.ActivationFunctionType
AX = mybir.AxisListType

P = 128
Q = 32
SMALL = (1, 2, 4, 8, 16)


def gated_delta_moe_kernel(nc, ins, consts, out):
    x = ins["L0_attn_x"]
    B, T, D = x.shape
    NC = T // P
    E = ins["L0_ffn_w_router"].shape[0]
    HID = ins["L0_ffn_w_gate"].shape[0]
    KH = HID // P
    CAPACITY = -(-(B * T * 5) // (4 * E))
    KVW = 2 * P + 1
    NS = len(SMALL)
    NR = NS + 2
    QUADS = P // Q
    assert D == P and T % P == 0 and B % 2 == 0 and B >= 4 and E == 8

    with ExitStack() as ctx:
        def sb(name, shape, dt=F32):
            return ctx.enter_context(nc.sbuf_tensor(name, shape, dt))

        def bank(name):
            return ctx.enter_context(nc.psum_tensor(name, [P, 512], F32))

        def sem(name):
            return ctx.enter_context(nc.semaphore(name))

        eye = sb("eye", [P, NC, P])
        eye_c = sb("eye_c", [P, NC, Q])
        pair_mask = sb("pair_mask", [P, NS, Q])
        prio = sb("prio", [P, NC, E])
        prefix = sb("prefix", [P, 2, P])
        prefix16 = sb("prefix16", [P, 2, P], BF16)
        wq = sb("wq", [P, P])
        wg = sb("wg", [P, P])
        wa_col = sb("wa_col", [P, 1])
        wa_rep = sb("wa_rep", [P, P])
        wkvb = sb("wkvb", [P, KVW])
        kvb_bias = sb("kvb_bias", [P, KVW])
        wo = sb("wo", [P, P])
        bo_bc = sb("bo_bc", [P, P])
        bq_col = sb("bq_col", [P, 1])
        bg_col = sb("bg_col", [P, 1])
        ba_col = sb("ba_col", [P, 1])
        w_router = sb("w_router", [P, E])
        w_gate = sb("w_gate", [P, HID])
        w_down = sb("w_down", [P, KH, E, P])
        pad = sb("pad", [P, 4])
        neg_half = sb("neg_half", [P, NC])

        xin = [sb(f"xin{p}", [P, NC, P]) for p in range(2)]
        a_st = sb("a_st", [P, NC, 6])
        a_mv = sb("a_mv", [P, NC, 2])
        a_veps = sb("a_veps", [P, NC])
        a_rstd = sb("a_rstd", [P, NC])
        xn = sb("xn", [P, NC, P])
        xnT = sb("xnT", [P, T])
        alpha = sb("alpha", [P, NC, P])
        alpha0 = sb("alpha0", [P, T + 8])
        alpha_first = sb("alpha_first", [P, T])
        decay_row = [sb(f"decay_row{p}", [P, T]) for p in range(2)]
        gam = sb("gam", [P, T])
        gamT = [sb(f"gamT{p}", [P, T]) for p in range(2)]
        kvb = sb("kvb", [P, NC, KVW + 3])
        ksq = sb("ksq", [P, NC, P])
        kss = sb("kss", [P, NC])
        kss_c = sb("kss_c", [P, NC])
        krn = sb("krn", [P, NC])
        beta = sb("beta", [P, NC])
        decay_col = sb("decay_col", [P, NC])
        neg_ba = [sb(f"neg_ba{p}", [P, NC]) for p in range(2)]
        kn = [sb(f"kn{p}", [P, NC, P]) for p in range(2)]
        kg = [sb(f"kg{p}", [P, NC, P]) for p in range(2)]
        bv = [sb(f"bv{p}", [P, NC, P]) for p in range(2)]
        kT = [sb(f"kT{p}", [P, T]) for p in range(2)]
        qT = [sb(f"qT{p}", [P, T]) for p in range(2)]
        qaT = [sb(f"qaT{p}", [P, T]) for p in range(2)]
        gT = [sb(f"gT{p}", [P, T]) for p in range(2)]
        Lbd = sb("Lbd", [P, NC, P])
        L32 = sb("L32", [P, NC, P])
        L64 = sb("L64", [P, NC, P])
        gamb = sb("gamb", [P, NC, P])
        Zc = sb("Zc", [P, NC, Q])
        Xc = sb("Xc", [P, NC, Q])
        Rc = sb("Rc", [P, NC, Q])
        R64 = sb("R64", [P, NC, 2 * Q])
        Xf = sb("Xf", [P, NC, P])
        X64 = sb("X64", [P, NC, P])
        Zf = [sb(f"Zf{p}", [P, NC, P]) for p in range(2)]

        state = [sb(f"state{p}", [P, 2, P]) for p in range(2)]
        rhs = sb("rhs", [P, P])
        w_wT = sb("w_wT", [P, 2, P])
        pT = sb("pT", [P, P])
        og = sb("og", [P, NC, P])
        x1 = [sb(f"x1_{p}", [P, NC, P]) for p in range(2)]
        c_st = sb("c_st", [P, NC, 6])
        c_mv = sb("c_mv", [P, NC, 2])
        c_veps = sb("c_veps", [P, NC])
        c_rstd = sb("c_rstd", [P, NC])
        xn2 = sb("xn2", [P, NC, P])
        xn2T = sb("xn2T", [P, T])
        sig_h = sb("sig_h", [P, KH, T])
        hT = [sb(f"hT{p}", [P, KH, T]) for p in range(2)]
        lg = sb("lg", [P, NC, E])
        top = sb("top", [P, 4, NC])
        rt = [sb(f"rt{n}", [P, NC, E]) for n in range(10)]
        mask16 = sb("mask16", [P, NC, E], BF16)
        before = sb("before", [P, NC + 1, E])
        before16 = sb("before16", [P, NC, E], BF16)
        sums = sb("sums", [P, 4, NC])
        comb = [sb(f"comb{p}", [P, NC, E]) for p in range(2)]

        psA, psK, psR, psZ, psB0, psB1 = [bank(n) for n in ("psA", "psK", "psR", "psZ", "psB0", "psB1")]
        psF = [bank("psF0"), bank("psF1")]

        names = """w_loaded pool_consts act_consts dve_consts
            a_stats a_aggr a_veps_ready a_rstd_ready xn_ready
            xnT_ps xnT_ready alpha_ps alpha_ready kv_ps kv_ready kss_ready kssc_ready krn_ready beta_ready
            alpha0_ready gam_ready decay_ready dcol_ready kn_ready kg_ready bv_ready negba_ready
            kT_ps kT_ready q_ps q_ready qa_ready g_ps g_ready kk_ps L_ready gamb_ready R_ps R_ready Z_ps
            Zc_ready Xc_ready X_ready X64_ps X64_ready Zd_ready Zo_ready
            rhs_ps rhs_ready w_ps w_ready qw_ps p_ready s_ps s_ready o_ps og_ready
            y_ps res_ready x1_ready c_stats c_aggr c_veps_ready c_rstd_ready xn2_ready xn2T_ps xn2T_ready
            log_ps log_ready h_ps sigh_ready h_ready route soft mask_ready cum_ps sig_ready comb_ready
            f_ps f_done f_acc""".split()
        s = {n: sem(n) for n in names}
        S = type("Sems", (), s)
        x_loaded = [sem(f"x_loaded{p}") for p in range(2)]
        res_loaded = [sem(f"res_loaded{p}") for p in range(2)]
        y_stored = [sem(f"y_stored{p}") for p in range(2)]

        block = ctx.enter_context(nc.Block())

        def wait(eng, sm, n):
            if not (isinstance(n, int) and n <= 0):
                eng.wait_ge(sm, n)

        LEAD = 4

        def batches(eng, iteration):
            def step(i):
                iteration(*[(n, n // 2, n % 2) if 0 <= n < B else None for n in (i, i - 1, i - 2)])

            for i in range(LEAD):
                step(i)
            with eng.Fori(0, (B - LEAD) // 2) as j:
                for k in range(2):
                    iteration(*[(2 * j + (m := LEAD + k - lag), j + m // 2, m % 2) for lag in range(3)])
            for i in range(B, B + 2):
                step(i)

        def ch(t, c):
            return t[:, c * P:(c + 1) * P]

        def flat(t):
            return t[:, :, :].rearrange("p c d -> p (c d)")

        N_LOADS = 20

        @block.sync
        def _(sp):
            col = lambda ap: ap.rearrange("(d o) -> d o", o=1)
            loads = [
                (wq[:, :], ins["L0_attn_Wq"]), (wg[:, :], ins["L0_attn_Wg"]), (wa_col[:, :], ins["L0_attn_Wa"]),
                (wkvb[:, 0:P], ins["L0_attn_Wk"]), (wkvb[:, P:2 * P], ins["L0_attn_Wv"]),
                (wkvb[:, 2 * P:KVW], ins["L0_attn_Wb"]),
                (kvb_bias[:, 0:P], ins["L0_attn_bk"].partition_broadcast(P)),
                (kvb_bias[:, P:2 * P], ins["L0_attn_bv"].partition_broadcast(P)),
                (kvb_bias[:, 2 * P:KVW], ins["L0_attn_bb"].partition_broadcast(P)),
                (bq_col[:, :], col(ins["L0_attn_bq"])), (bg_col[:, :], col(ins["L0_attn_bg"])),
                (ba_col[:, :], ins["L0_attn_ba"].partition_broadcast(P)),
                (bo_bc[:, :], ins["L0_attn_bo"].partition_broadcast(P)),
                (eye[:, :, :], consts["eye"]), (eye_c[:, :, :], consts["eye_c"]),
                (pair_mask[:, :, :], consts["pair_mask"]), (prefix[:, :, :], consts["prefix"]),
                (wo[:, :], ins["L0_attn_Wo"]), (w_router[:, :], ins["w_router_T"]),
                (w_gate[:, :], ins["w_gate_T"]),
            ]
            assert len(loads) == N_LOADS
            sp.dma_start(xin[0][:, :, :], x[0].rearrange("(c p) d -> p c d", p=P)).then_inc(x_loaded[0], 16)
            for dst, src in loads:
                sp.dma_start(dst, src).then_inc(S.w_loaded, 16)
            sp.dma_start(w_down[:, :, :, :], ins["w_down_T"].rearrange("(k p) e d -> p k e d", p=P)).then_inc(S.w_loaded, 16)
            sp.dma_start(prio[:, :, :], consts["prio"]).then_inc(S.w_loaded, 16)

            def iteration(b0, b1, b2):
                def load(b):
                    n, h, p = b
                    if isinstance(n, int) and n == 0:
                        return
                    wait(sp, S.xn_ready, NC * (n - 1))
                    sp.dma_start(xin[p][:, :, :], x[n].rearrange("(c p) d -> p c d", p=P)).then_inc(x_loaded[p], 16)

                def load_residual(b):
                    n, h, p = b
                    wait(sp, y_stored[p], 16 * h)
                    sp.dma_start(x1[p][:, :, :], x[n].rearrange("(c p) d -> p c d", p=P)).then_inc(res_loaded[p], 16)

                def store(b):
                    n, h, p = b
                    sp.wait_ge(S.f_acc, NC * E * (n + 1))
                    sp.dma_start(out[n].rearrange("(c p) d -> p c d", p=P), x1[p][:, :, :]).then_inc(y_stored[p], 16)

                if b0: load(b0)
                if b2: store(b2)
                if b0: load_residual(b0)

            batches(sp, iteration)
            for p in range(2):
                sp.wait_ge(y_stored[p], 16 * (B // 2))

        W_ALL = 16 * (N_LOADS + 2)

        @block.gpsimd
        def _(pool):
            pool.memset(neg_half[:, :], -0.5).then_inc(S.pool_consts, 1)
            pool.wait_ge(S.w_loaded, W_ALL)
            pool.wait_ge(S.pool_consts, 1)

            def iteration(b0, b1, b2):
                def a_rstd_pow(b):
                    n, h, p = b
                    pool.wait_ge(S.a_veps_ready, n + 1)
                    pool.tensor_tensor(a_rstd[:, :], a_veps[:, :], neg_half[:, :], ALU.pow).then_inc(S.a_rstd_ready, 1)

                def a_krn(b):
                    n, h, p = b
                    pool.wait_ge(S.kssc_ready, n + 1)
                    pool.tensor_tensor(krn[:, :], kss_c[:, :], neg_half[:, :], ALU.pow).then_inc(S.krn_ready, 1)

                def a_qa(b):
                    n, h, p = b
                    pool.wait_ge(S.q_ready, n + 1)
                    pool.wait_ge(S.decay_ready, n + 1)
                    wait(pool, S.og_ready, NC * (n - 1))
                    pool.tensor_tensor(qaT[p][:, :], qT[p][:, :], decay_row[p][:, :], ALU.mult).then_inc(S.qa_ready, 1)

                def c_bias(b):
                    n, h, p = b
                    pool.wait_ge(res_loaded[p], 16 * (h + 1))
                    pool.tensor_tensor(x1[p][:, :, :], x1[p][:, :, :],
                                       bo_bc[:, :].unsqueeze(1).to_broadcast([P, NC, P]), ALU.add).then_inc(S.res_ready, 1)

                def c_rstd_pow(b):
                    n, h, p = b
                    pool.wait_ge(S.c_veps_ready, n + 1)
                    pool.tensor_tensor(c_rstd[:, :], c_veps[:, :], neg_half[:, :], ALU.pow).then_inc(S.c_rstd_ready, 1)

                if b1: a_krn(b1)
                if b0: a_rstd_pow(b0)
                if b2: c_rstd_pow(b2)
                if b1: a_qa(b1); c_bias(b1)

            batches(pool, iteration)

        @block.scalar
        def _(act):
            act.wait_ge(S.w_loaded, W_ALL)
            act.wait_ge(S.dve_consts, 9)
            nc.scalar.activation(prefix16[:, :, :], prefix[:, :, :], ACT.Copy).then_inc(S.act_consts, 1)
            nc.scalar.activation(wa_rep[:, :], wa_col[:, :].to_broadcast([P, P]), ACT.Copy).then_inc(S.act_consts, 1)

            def iteration(b0, b1, b2):
                def w_copy(b, c):
                    n, h, p = b
                    m = NC * n + c
                    act.wait_ge(S.w_ps, m + 1)
                    wait(act, S.og_ready, m)
                    act.activation(w_wT[:, :, :], psB0[:, P:3 * P].rearrange("p (a d) -> p a d", a=2), ACT.Copy).then_inc(S.w_ready, 1)

                def expand_x(b, l):
                    n, h, p = b
                    act.wait_ge(S.Xc_ready, NS * n + l + 1)
                    wait(act, S.Z_ps, (NR - 1) * n + l)
                    for g in range(QUADS):
                        rows = slice(g * Q, g * Q + Q)
                        act.activation(Xf[rows, :, rows], Xc[rows, :, :], ACT.Copy).then_inc(S.X_ready, 1)

                def scaled(dst, src, by, done):
                    for c in range(NC):
                        act.activation(dst[:, c, :], src(c), ACT.Copy, scale=by(c)).then_inc(done, 1)

                def z_diag(b):
                    n, h, p = b
                    wait(act, S.w_ps, NC * (n - 1))
                    for g in range(QUADS):
                        rows = slice(g * Q, g * Q + Q)
                        act.activation(Zf[p][rows, :, rows], Zc[rows, :, :], ACT.Copy).then_inc(S.Zd_ready, 1)

                def r_big(b, l, dst, w):
                    n, h, p = b
                    act.wait_ge(S.R_ps, NR * n + l + 1)
                    act.activation(dst[:, :, :], psR[:, 0:NC * w].rearrange("p (c t) -> p c t", c=NC), ACT.Copy,
                                   scale=-1.0).then_inc(S.R_ready, 1)

                def z_off32(b):
                    n, h, p = b
                    act.wait_ge(S.Z_ps, (NR - 1) * n + NS)
                    for g in (0, 2):
                        act.activation(Zf[p][g * Q:g * Q + Q, :, g * Q + Q:g * Q + 2 * Q],
                                       psZ[g * Q:g * Q + Q, 0:NC * Q].rearrange("p (c t) -> p c t", c=NC),
                                       ACT.Copy).then_inc(S.Zo_ready, 1)

                def x64(b):
                    n, h, p = b
                    act.wait_ge(S.X64_ps, n + 1)
                    act.activation(flat(X64), psZ[:, :], ACT.Copy).then_inc(S.X64_ready, 1)

                def z_off64(b):
                    n, h, p = b
                    act.wait_ge(S.Z_ps, (NR - 1) * (n + 1))
                    act.activation(Zf[p][0:2 * Q, :, 2 * Q:P],
                                   psZ[0:2 * Q, 0:NC * 2 * Q].rearrange("p (c t) -> p c t", c=NC),
                                   ACT.Copy).then_inc(S.Zo_ready, 1)

                def a_xnT(b):
                    n, h, p = b
                    act.wait_ge(S.xnT_ps, n + 1)
                    act.activation(xnT[:, :], psA[:, :], ACT.Copy).then_inc(S.xnT_ready, 1)

                def a_alpha(b):
                    n, h, p = b
                    act.wait_ge(S.alpha_ps, n + 1)
                    wait(act, S.dcol_ready, n)
                    act.activation(flat(alpha), psK[:, :], ACT.Sigmoid, bias=ba_col[:, 0:1]).then_inc(S.alpha_ready, 1)

                def a_kss(b):
                    n, h, p = b
                    for c in range(NC):
                        act.wait_ge(S.kv_ready, NC * n + c + 1)
                        act.activation(ksq[:, c, :], kvb[:, c, 0:P], ACT.Square, accum_out=kss[:, c:c + 1]).then_inc(S.kss_ready, 1)
                    wait(act, S.negba_ready, n)
                    act.activation(beta[:, :], kvb[:, :, 2 * P], ACT.Sigmoid).then_inc(S.beta_ready, 1)

                def a_gamb(b):
                    n, h, p = b
                    act.wait_ge(S.beta_ready, n + 1)
                    act.wait_ge(S.gam_ready, 2 * n + 1)
                    wait(act, S.L_ready, 7 * n)
                    scaled(gamb, lambda c: ch(gam, c), lambda c: beta[:, c:c + 1], S.gamb_ready)

                def a_kT(b):
                    n, h, p = b
                    act.wait_ge(S.kT_ps, n + 1)
                    wait(act, S.w_ps, NC * (n - 1))
                    act.activation(kT[p][:, :], psA[:, :], ACT.Copy).then_inc(S.kT_ready, 1)

                def a_q(b):
                    n, h, p = b
                    act.wait_ge(S.q_ps, n + 1)
                    act.activation(qT[p][:, :], psA[:, :], ACT.Identity, bias=bq_col[:, 0:1]).then_inc(S.q_ready, 1)

                def a_g(b):
                    n, h, p = b
                    act.wait_ge(S.g_ps, n + 1)
                    act.activation(gT[p][:, :], psK[:, :], ACT.Sigmoid, bias=bg_col[:, 0:1]).then_inc(S.g_ready, 1)

                def a_bv(b):
                    n, h, p = b
                    scaled(bv[p], lambda c: kvb[:, c, P:2 * P], lambda c: beta[:, c:c + 1], S.bv_ready)

                def a_kg(b):
                    n, h, p = b
                    scaled(kg[p], lambda c: kn[p][:, c, :], lambda c: gamT[p][:, c * P + P - 1:c * P + P], S.kg_ready)

                def c_xnT(b):
                    n, h, p = b
                    act.wait_ge(S.xn2T_ps, n + 1)
                    act.activation(xn2T[:, :], psB1[:, :], ACT.Copy).then_inc(S.xn2T_ready, 1)

                def c_sigh(b, k):
                    n, h, p = b
                    act.wait_ge(S.h_ps, KH * n + k + 1)
                    wait(act, S.h_ready, KH * (n - 1) + k + 1)
                    act.activation(sig_h[:, k, :], (psB0 if k else psB1)[:, :], ACT.Sigmoid).then_inc(S.sigh_ready, 1)

                def c_soft(b):
                    n, h, p = b
                    act.wait_ge(S.soft, 2 * n + 1)
                    act.activation(rt[6][:, :, :], rt[5][:, :, :], ACT.Sigmoid).then_inc(S.sig_ready, 1)
                    act.activation(rt[7][:, :, :], rt[5][:, :, :], ACT.Sigmoid, scale=-1.0).then_inc(S.sig_ready, 1)

                if b2: w_copy(b2, 3)
                if b1: expand_x(b1, 2); a_q(b1)
                if b0: a_xnT(b0)
                if b1: expand_x(b1, 3)
                if b0: a_alpha(b0)
                if b1: expand_x(b1, 4); r_big(b1, NS, Rc, Q)
                if b2: c_xnT(b2)
                if b1: z_diag(b1); z_off32(b1); x64(b1)
                if b2: c_sigh(b2, 0); c_sigh(b2, 1); c_soft(b2)
                if b1: r_big(b1, NS + 1, R64, 2 * Q); z_off64(b1)
                if b0: a_kss(b0)
                if b1: w_copy(b1, 0)
                if b0: a_gamb(b0); a_bv(b0); a_kT(b0)
                if b1: w_copy(b1, 1)
                if b0: expand_x(b0, 0)
                if b1: w_copy(b1, 2)
                if b0: expand_x(b0, 1); a_g(b0); a_kg(b0)

            batches(act, iteration)

        @block.vector
        def _(dve):
            dve.memset(alpha0[:, :], 0.0).then_inc(S.dve_consts, 1)
            dve.memset(alpha_first[:, :], 0.0).then_inc(S.dve_consts, 1)
            dve.memset(before[:, :, :], 0.0).then_inc(S.dve_consts, 1)
            for t in (Lbd, L32, L64, Xf, *Zf):
                dve.memset(t[:, :, :], 0.0).then_inc(S.dve_consts, 1)
            dve.wait_ge(S.w_loaded, W_ALL)
            dve.wait_ge(S.dve_consts, 9)

            def iteration(b0, b1, b2):
                def a_norm(b):
                    n, h, p = b
                    dve.wait_ge(x_loaded[p], 16 * (h + 1))
                    for c in range(NC):
                        dve.bn_stats(a_st[:, c, :], xin[p][:, c, :]).then_inc(S.a_stats, 1)
                    dve.wait_ge(S.a_stats, NC * (n + 1))
                    dve.memset(pad[:, 0:1], 0.0)
                    for c in range(NC):
                        dve.bn_aggr(a_mv[:, c, :], a_st[:, c, :]).then_inc(S.a_aggr, 1)
                    dve.wait_ge(S.a_aggr, NC * (n + 1))
                    dve.tensor_scalar(a_veps[:, :], a_mv[:, :, 1], 1e-5, None, ALU.add).then_inc(S.a_veps_ready, 1)

                def a_xn(b):
                    n, h, p = b
                    dve.wait_ge(S.a_rstd_ready, n + 1)
                    for c in range(NC):
                        dve.tensor_scalar(xn[:, c, :], xin[p][:, c, :], a_mv[:, c, 0:1], a_rstd[:, c:c + 1],
                                          ALU.subtract, ALU.mult).then_inc(S.xn_ready, 1)

                def a_kv(b, c):
                    n, h, p = b
                    dve.wait_ge(S.kv_ps, NC * n + c + 1)
                    dve.tensor_tensor(kvb[:, c, 0:KVW], (psK if c % 2 else psA)[:, 0:KVW], kvb_bias[:, :], ALU.add).then_inc(S.kv_ready, 1)

                def a_decay(b):
                    n, h, p = b
                    dve.wait_ge(S.alpha_ready, n + 1)
                    dve.tensor_copy(alpha0[:, 0:T].rearrange("p (c t) -> p c t", c=NC)[:, :, 1:P],
                                    alpha[:, :, 1:P]).then_inc(S.alpha0_ready, 1)
                    dve.tensor_copy(alpha_first[:, :].rearrange("p (c t) -> p c t", c=NC)[:, :, 0],
                                    alpha[:, :, 0]).then_inc(S.alpha0_ready, 1)
                    dve.wait_ge(S.alpha0_ready, 2 * (n + 1))
                    wait(dve, S.gamb_ready, NC * n)
                    dve.tensor_tensor_scan(gam[:, ::-1], alpha0[:, 1:T + 1][:, ::-1], flat(eye)[:, ::-1], 0.0,
                                           ALU.mult, ALU.add).then_inc(S.gam_ready, 1)
                    wait(dve, S.og_ready, NC * (n - 1))
                    dve.tensor_tensor_scan(gamT[p][:, :], alpha0[:, 0:T], flat(eye), 0.0,
                                           ALU.mult, ALU.add).then_inc(S.gam_ready, 1)
                    dve.tensor_tensor_scan(decay_row[p][:, :], alpha0[:, 0:T], alpha_first[:, :], 0.0,
                                           ALU.mult, ALU.add).then_inc(S.decay_ready, 1)
                    dve.wait_ge(S.gam_ready, 2 * (n + 1))
                    dve.tensor_tensor(decay_col[:, :], gam[:, :].rearrange("p (c t) -> p c t", c=NC)[:, :, 0],
                                      alpha[:, :, 0], ALU.mult).then_inc(S.dcol_ready, 1)

                def a_knorm(b):
                    n, h, p = b
                    dve.wait_ge(S.kss_ready, NC * (n + 1))
                    dve.tensor_scalar(kss_c[:, :], kss[:, :], 1e-24, None, ALU.max).then_inc(S.kssc_ready, 1)

                def a_negba(b):
                    n, h, p = b
                    dve.wait_ge(S.beta_ready, n + 1)
                    dve.wait_ge(S.dcol_ready, n + 1)
                    wait(dve, S.rhs_ready, (NC - 1) * (n - 1))
                    dve.scalar_tensor_tensor(neg_ba[p][:, :], decay_col[:, :], -1.0, beta[:, :],
                                             ALU.mult, ALU.mult).then_inc(S.negba_ready, 1)

                def a_keys(b):
                    n, h, p = b
                    dve.wait_ge(S.krn_ready, n + 1)
                    dve.tensor_tensor(kn[p][:, :, :], kvb[:, :, 0:P], krn[:, :].unsqueeze(2).to_broadcast([P, NC, P]),
                                      ALU.mult).then_inc(S.kn_ready, 1)

                def a_L(b):
                    n, h, p = b
                    dve.wait_ge(S.kk_ps, n + 1)
                    dve.wait_ge(S.gamb_ready, NC * (n + 1))
                    wait(dve, S.R_ps, NR * n)
                    kk = psR[:, :].rearrange("p (c t) -> p c t", c=NC)
                    parts = [(Lbd, slice(g * Q, g * Q + Q), slice(g * Q, g * Q + Q)) for g in range(QUADS)]
                    parts += [(L32, slice(g * Q, g * Q + Q), slice(g * Q - Q, g * Q)) for g in (1, 3)]
                    parts += [(L64, slice(2 * Q, P), slice(0, 2 * Q))]
                    for dst, rows, cols in parts:
                        dve.tensor_tensor(dst[rows, :, cols], kk[rows, :, cols], gamb[rows, :, cols],
                                          ALU.mult).then_inc(S.L_ready, 1)

                def a_R(b, l):
                    n, h, p = b
                    dve.wait_ge(S.R_ps, NR * n + l + 1)
                    dve.tensor_tensor(Rc[:, :, :], psR[:, 0:NC * Q].rearrange("p (c t) -> p c t", c=NC),
                                      pair_mask[:, l, :].unsqueeze(1).to_broadcast([P, NC, Q]), ALU.mult).then_inc(S.R_ready, 1)

                def a_Z(b, l):
                    n, h, p = b
                    if l == 0:
                        dve.wait_ge(S.R_ready, NR * n + 1)
                        wait(dve, S.Zd_ready, QUADS * n)
                        dve.tensor_tensor(Zc[:, :, :], eye_c[:, :, :], Rc[:, :, :], ALU.add).then_inc(S.Zc_ready, 1)
                    else:
                        dve.wait_ge(S.Z_ps, (NR - 1) * n + l)
                        dve.tensor_tensor(Zc[:, :, :], Zc[:, :, :], psZ[:, 0:NC * Q].rearrange("p (c t) -> p c t", c=NC),
                                          ALU.add).then_inc(S.Zc_ready, 1)
                    dve.wait_ge(S.Zc_ready, NS * n + l + 1)
                    wait(dve, S.X_ready, QUADS * (NS * n + l))
                    dve.transpose(Xc[:, :, :].rearrange("p c t -> p (c t)"),
                                  Zc[:, :, :].rearrange("p c t -> p (c t)")).then_inc(S.Xc_ready, 1)

                def b_rhs(b, c):
                    n, h, p = b
                    dve.wait_ge(S.rhs_ps, (NC - 1) * n + c)
                    dve.scalar_tensor_tensor(rhs[:, :], psB0[:, 0:P], neg_ba[p][:, c:c + 1], bv[p][:, c, :],
                                             ALU.mult, ALU.add).then_inc(S.rhs_ready, 1)

                def b_p(b, c):
                    n, h, p = b
                    dve.wait_ge(S.qw_ps, NC * n + c + 1)
                    dve.tensor_tensor(pT[:, :], psB0[:, 3 * P:4 * P], ch(gamT[p], c), ALU.mult).then_inc(S.p_ready, 1)

                def b_state(b, c):
                    n, h, p = b
                    m = (NC - 1) * n + c
                    dve.wait_ge(S.s_ps, m + 1)
                    both = psB1[:, 0:2 * P].rearrange("p (a d) -> p a d", a=2)
                    if c == 0:
                        dve.tensor_copy(state[1][:, :, :], both).then_inc(S.s_ready, 1)
                    else:
                        dve.wait_ge(S.s_ready, m)
                        dve.scalar_tensor_tensor(state[(c + 1) % 2][:, :, :], state[c % 2][:, :, :],
                                                 decay_row[p][:, c * P + P - 1:c * P + P], both,
                                                 ALU.mult, ALU.add).then_inc(S.s_ready, 1)

                def b_o(b, c):
                    n, h, p = b
                    dve.wait_ge(S.o_ps, NC * n + c + 1)
                    dve.tensor_tensor(og[:, c, :], psB1[:, 2 * P:3 * P], ch(gT[p], c), ALU.mult).then_inc(S.og_ready, 1)

                def c_norm(b):
                    n, h, p = b
                    dve.wait_ge(S.y_ps, n + 1)
                    dve.wait_ge(S.res_ready, n + 1)
                    dve.tensor_tensor(flat(x1[p]), psB0[:, :], flat(x1[p]), ALU.add).then_inc(S.x1_ready, 1)
                    dve.wait_ge(S.x1_ready, n + 1)
                    for c in range(NC):
                        dve.bn_stats(c_st[:, c, :], x1[p][:, c, :]).then_inc(S.c_stats, 1)
                    dve.wait_ge(S.c_stats, NC * (n + 1))
                    dve.memset(pad[:, 1:2], 0.0)
                    for c in range(NC):
                        dve.bn_aggr(c_mv[:, c, :], c_st[:, c, :]).then_inc(S.c_aggr, 1)
                    dve.wait_ge(S.c_aggr, NC * (n + 1))
                    dve.tensor_scalar(c_veps[:, :], c_mv[:, :, 1], 1e-5, None, ALU.add).then_inc(S.c_veps_ready, 1)

                def c_xn(b):
                    n, h, p = b
                    dve.wait_ge(S.c_rstd_ready, n + 1)
                    for c in range(NC):
                        dve.tensor_scalar(xn2[:, c, :], x1[p][:, c, :], c_mv[:, c, 0:1], c_rstd[:, c:c + 1],
                                          ALU.subtract, ALU.mult).then_inc(S.xn2_ready, 1)

                def c_h(b, k):
                    n, h, p = b
                    dve.wait_ge(S.sigh_ready, KH * n + k + 1)
                    wait(dve, S.f_acc, NC * E * (n - 1))
                    dve.tensor_tensor(hT[p][:, k, :], (psB0 if k else psB1)[:, :], sig_h[:, k, :],
                                      ALU.mult).then_inc(S.h_ready, 1)

                STEPS = 12

                def bc(t):
                    return t.unsqueeze(2).to_broadcast([P, NC, E])

                def c_logits(b):
                    n, h, p = b
                    dve.wait_ge(S.log_ps, n + 1)
                    dve.tensor_copy(lg[:, :, :], psB0[:, 0:NC * E].rearrange("p (c e) -> p c e", c=NC)).then_inc(S.route, 1)

                def c_top2(b):
                    n, h, p = b
                    def step(k, ins_):
                        ins_.then_inc(S.route, 1)
                        dve.wait_ge(S.route, STEPS * n + k)
                    dve.wait_ge(S.route, STEPS * n + 1)
                    step(2, dve.tensor_reduce(top[:, 0, :], lg[:, :, :], AX.X, ALU.max))
                    dve.tensor_tensor(rt[5][:, :, :], lg[:, :, :], bc(top[:, 0, :]), ALU.subtract).then_inc(S.soft, 1)
                    step(3, dve.tensor_tensor(rt[0][:, :, :], lg[:, :, :], bc(top[:, 0, :]), ALU.is_equal))
                    step(4, dve.tensor_tensor(rt[0][:, :, :], rt[0][:, :, :], prio[:, :, :], ALU.mult))
                    step(5, dve.tensor_reduce(top[:, 1, :], rt[0][:, :, :], AX.X, ALU.max))
                    step(6, dve.tensor_tensor(rt[1][:, :, :], prio[:, :, :], bc(top[:, 1, :]), ALU.is_equal))
                    step(7, dve.scalar_tensor_tensor(rt[2][:, :, :], rt[1][:, :, :], -3e38, lg[:, :, :], ALU.mult, ALU.add))
                    step(8, dve.tensor_reduce(top[:, 2, :], rt[2][:, :, :], AX.X, ALU.max))
                    step(9, dve.tensor_tensor(rt[3][:, :, :], rt[2][:, :, :], bc(top[:, 2, :]), ALU.is_equal))
                    step(10, dve.tensor_tensor(rt[3][:, :, :], rt[3][:, :, :], prio[:, :, :], ALU.mult))
                    step(11, dve.tensor_reduce(top[:, 3, :], rt[3][:, :, :], AX.X, ALU.max))
                    step(12, dve.tensor_tensor(rt[4][:, :, :], prio[:, :, :], bc(top[:, 3, :]), ALU.is_equal))
                    dve.tensor_tensor(mask16[:, :, :], rt[4][:, :, :], rt[1][:, :, :], ALU.add).then_inc(S.mask_ready, 1)
                    dve.tensor_tensor(rt[8][:, :, :], rt[4][:, :, :], rt[1][:, :, :], ALU.add).then_inc(S.mask_ready, 1)
                    dve.wait_ge(S.mask_ready, 9 * n + 2)
                    for c in range(NC):
                        dve.tensor_tensor(before[:, c + 1, :], before[:, c, :], rt[8][:, c, :], ALU.add).then_inc(S.mask_ready, 1)
                        dve.wait_ge(S.mask_ready, 9 * n + 3 + c)
                    dve.tensor_copy(before16[:, :, :], before[:, 0:NC, :]).then_inc(S.mask_ready, 1)
                    dve.wait_ge(S.mask_ready, 9 * n + 7)
                    dve.tensor_copy(before[:, 0, :], before[:, NC, :]).then_inc(S.mask_ready, 1)
                    dve.wait_ge(S.mask_ready, 9 * n + 8)
                    dve.memset(sums[:, 0, 0:1], 0.0).then_inc(S.mask_ready, 1)

                CS = 9

                def c_comb(b):
                    n, h, p = b
                    def step(k, ins_):
                        ins_.then_inc(S.comb_ready, 1)
                        dve.wait_ge(S.comb_ready, CS * n + k)
                    dve.wait_ge(S.sig_ready, 2 * (n + 1))
                    step(1, dve.reciprocal(rt[9][:, :, :], rt[7][:, :, :]))
                    step(2, dve.tensor_tensor(rt[6][:, :, :], rt[6][:, :, :], rt[9][:, :, :], ALU.mult))
                    step(3, dve.tensor_reduce(sums[:, 0, :], rt[6][:, :, :], AX.X, ALU.add))
                    step(4, dve.reciprocal(sums[:, 1, :], sums[:, 0, :]))
                    dve.wait_ge(S.cum_ps, n + 1)
                    step(5, dve.scalar_tensor_tensor(rt[2][:, :, :], psB1[:, 0:NC * E].rearrange("p (c e) -> p c e", c=NC),
                                                     float(CAPACITY), rt[8][:, :, :], ALU.is_le, ALU.mult))
                    step(6, dve.tensor_tensor(rt[2][:, :, :], rt[2][:, :, :], rt[6][:, :, :], ALU.mult))
                    step(7, dve.tensor_tensor(rt[2][:, :, :], rt[2][:, :, :], bc(sums[:, 1, :]), ALU.mult))
                    step(8, dve.tensor_reduce(sums[:, 2, :], rt[2][:, :, :], AX.X, ALU.add))
                    dve.tensor_scalar(sums[:, 3, :], sums[:, 2, :], 1e-6, None, ALU.add).then_inc(S.soft, 1)
                    dve.wait_ge(S.soft, 2 * (n + 1))
                    dve.reciprocal(top[:, 0, :], sums[:, 3, :]).then_inc(S.log_ready, 1)
                    dve.wait_ge(S.log_ready, n + 1)
                    wait(dve, S.f_acc, NC * E * (n - 1))
                    step(9, dve.tensor_tensor(comb[p][:, :, :], rt[2][:, :, :], bc(top[:, 0, :]), ALU.mult))

                def f_sum(b, c, half):
                    n, h, p = b
                    dve.wait_ge(S.f_ps, 2 * NC * n + 2 * c + half + 1)
                    for e in range(4):
                        if c or half or e:
                            dve.wait_ge(S.f_acc, NC * E * n + E * c + 4 * half + e)
                        dve.scalar_tensor_tensor(x1[p][:, c, :], psF[half][:, e * P:(e + 1) * P],
                                                 comb[p][:, c, 4 * half + e:4 * half + e + 1], x1[p][:, c, :],
                                                 ALU.mult, ALU.add).then_inc(S.f_acc, 1)

                if b0: a_norm(b0)
                if b1: a_Z(b1, 2)
                if b2: b_p(b2, 3)
                if b1: a_R(b1, 3)
                if b2: b_o(b2, 3)
                if b0: a_xn(b0)
                if b1: a_Z(b1, 3)
                if b2: c_norm(b2)
                if b1: a_R(b1, 4)
                if b0: a_kv(b0, 0)
                if b1: a_Z(b1, 4)
                if b2: c_xn(b2)
                if b0: a_kv(b0, 1); a_kv(b0, 2); a_kv(b0, 3)
                if b2: c_logits(b2); c_top2(b2); c_h(b2, 0); c_h(b2, 1); c_comb(b2)
                if b0: a_decay(b0); a_knorm(b0)
                if b2: f_sum(b2, 0, 0)
                if b1: b_state(b1, 0); b_p(b1, 0)
                if b0: a_keys(b0)
                if b1: b_o(b1, 0); b_rhs(b1, 1)
                if b2: f_sum(b2, 0, 1); f_sum(b2, 1, 0)
                if b0: a_L(b0); a_negba(b0)
                if b2: f_sum(b2, 1, 1)
                if b1: b_state(b1, 1); b_p(b1, 1)
                if b0: a_R(b0, 0)
                if b2: f_sum(b2, 2, 0)
                if b0: a_Z(b0, 0)
                if b1: b_rhs(b1, 2)
                if b0: a_R(b0, 1)
                if b1: b_o(b1, 1)
                if b2: f_sum(b2, 2, 1)
                if b0: a_Z(b0, 1)
                if b2: f_sum(b2, 3, 0)
                if b1: b_state(b1, 2); b_p(b1, 2)
                if b2: f_sum(b2, 3, 1)
                if b0: a_R(b0, 2)
                if b1: b_rhs(b1, 3); b_o(b1, 2)

            batches(dve, iteration)

        @block.tensor
        def _(pe):
            pe.wait_ge(S.w_loaded, W_ALL)
            pe.wait_ge(S.act_consts, 2)
            pe.wait_ge(S.dve_consts, 9)

            def mm(o, lhsT, r, start=True, stop=True):
                return nc.tensor.matmul(o, lhsT, r, start=start, stop=stop)

            def iteration(b0, b1, b2):
                def a_T(b):
                    n, h, p = b
                    wait(pe, S.q_ready, n)
                    for c in range(NC):
                        pe.wait_ge(S.xn_ready, NC * n + c + 1)
                        last = nc.tensor.transpose(psA[:, c * P:(c + 1) * P], xn[:, c, :], eye[:, 0, :])
                    last.then_inc(S.xnT_ps, 1)

                def a_alpha(b):
                    n, h, p = b
                    pe.wait_ge(S.xnT_ready, n + 1)
                    wait(pe, S.g_ready, n)
                    mm(psK[:, :], wa_rep[:, :], xnT[:, :]).then_inc(S.alpha_ps, 1)

                def a_kv(b, c):
                    n, h, p = b
                    if c == 0:
                        wait(pe, S.kn_ready, n)
                        wait(pe, S.bv_ready, NC * n)
                    elif c == 1:
                        pe.wait_ge(S.alpha_ready, n + 1)
                    else:
                        pe.wait_ge(S.kv_ready, NC * n + c - 1)
                    mm((psK if c % 2 else psA)[:, 0:KVW], xnT[:, c * P:(c + 1) * P], wkvb[:, :]).then_inc(S.kv_ps, 1)

                def a_kT(b):
                    n, h, p = b
                    pe.wait_ge(S.kn_ready, n + 1)
                    for c in range(NC):
                        last = nc.tensor.transpose(psA[:, c * P:(c + 1) * P], kn[p][:, c, :], eye[:, 0, :])
                    last.then_inc(S.kT_ps, 1)

                def a_kk(b):
                    n, h, p = b
                    pe.wait_ge(S.kT_ready, n + 1)
                    wait(pe, S.R_ready, NR * n)
                    for c in range(NC):
                        last = mm(psR[:, c * P:(c + 1) * P], ch(kT[p], c), ch(kT[p], c))
                    last.then_inc(S.kk_ps, 1)

                def a_q(b):
                    n, h, p = b
                    pe.wait_ge(S.kT_ready, n + 1)
                    mm(psA[:, :], wq[:, :], xnT[:, :]).then_inc(S.q_ps, 1)

                def a_g(b):
                    n, h, p = b
                    pe.wait_ge(S.kv_ready, NC * (n + 1))
                    mm(psK[:, :], wg[:, :], xnT[:, :]).then_inc(S.g_ps, 1)

                def a_R(b, l):
                    n, h, p = b
                    if l == 0:
                        pe.wait_ge(S.L_ready, 7 * (n + 1))
                    elif l <= NS:
                        pe.wait_ge(S.Zc_ready, NS * n + l)
                    else:
                        pe.wait_ge(S.Zo_ready, 3 * n + 2)
                    w = 2 * Q if l > NS else Q
                    for c in range(NC):
                        src = eye_c[:, c, :] if l == 0 else Zc[:, c, :] if l <= NS else Zf[p][:, c, 2 * Q:P]
                        last = mm(psR[:, c * w:(c + 1) * w], (Lbd, L32, L64)[max(0, l - NS + 1)][:, c, :], src)
                    last.then_inc(S.R_ps, 1)

                def a_Z(b, l):
                    n, h, p = b
                    pe.wait_ge(S.R_ready, NR * n + l + 1)
                    if l <= NS:
                        pe.wait_ge(S.X_ready, QUADS * (NS * n + l))
                        if l == 1:
                            wait(pe, S.Zo_ready, 3 * n)
                    else:
                        pe.wait_ge(S.X64_ready, n + 1)
                    w = 2 * Q if l > NS else Q
                    for c in range(NC):
                        last = mm(psZ[:, c * w:(c + 1) * w], (X64 if l > NS else Xf)[:, c, :],
                                  (R64 if l > NS else Rc)[:, c, :])
                    last.then_inc(S.Z_ps, 1)

                def a_X64(b):
                    n, h, p = b
                    pe.wait_ge(S.Zd_ready, QUADS * (n + 1))
                    pe.wait_ge(S.Zo_ready, 3 * n + 2)
                    for c in range(NC):
                        last = nc.tensor.transpose(psZ[:, c * P:(c + 1) * P], Zf[p][:, c, :], eye[:, 0, :])
                    last.then_inc(S.X64_ps, 1)

                def b_rhs(b, c):
                    n, h, p = b
                    pe.wait_ge(S.s_ready, (NC - 1) * n + c)
                    mm(psB0[:, 0:P], ch(kT[p], c), state[c % 2][:, 1, :]).then_inc(S.rhs_ps, 1)

                def b_w(b, c):
                    n, h, p = b
                    if c == 0:
                        pe.wait_ge(S.Zo_ready, 3 * (n + 1))
                        pe.wait_ge(S.bv_ready, NC * (n + 1))
                        wait(pe, S.h_ready, KH * n)
                        wait(pe, S.comb_ready, 9 * n)
                        r = bv[p][:, 0, :]
                    else:
                        pe.wait_ge(S.rhs_ready, (NC - 1) * n + c)
                        r = rhs[:, :]
                    mm(psB0[:, P:2 * P], Zf[p][:, c, :], r)
                    mm(psB0[:, 2 * P:3 * P], r, Zf[p][:, c, :]).then_inc(S.w_ps, 1)

                def b_qw_s(b, c):
                    n, h, p = b
                    m = NC * n + c
                    pe.wait_ge(S.w_ready, m + 1)
                    if c < NC - 1:
                        pe.wait_ge(S.kg_ready, NC * (n + 1))
                        if c:
                            pe.wait_ge(S.og_ready, m)
                        mm(psB1[:, 0:P], w_wT[:, 0, :], kg[p][:, c, :])
                        mm(psB1[:, P:2 * P], kg[p][:, c, :], w_wT[:, 0, :]).then_inc(S.s_ps, 1)
                    pe.wait_ge(S.q_ready, n + 1)
                    mm(psB0[:, 3 * P:4 * P], w_wT[:, 1, :], ch(qT[p], c)).then_inc(S.qw_ps, 1)

                def b_o(b, c):
                    n, h, p = b
                    m = NC * n + c
                    if c < NC - 1:
                        pe.wait_ge(S.s_ready, (NC - 1) * n + c + 1)
                    else:
                        pe.wait_ge(S.og_ready, m)
                    if c > 0:
                        pe.wait_ge(S.qa_ready, n + 1)
                        mm(psB1[:, 2 * P:3 * P], state[c % 2][:, 0, :], ch(qaT[p], c), stop=False)
                    pe.wait_ge(S.p_ready, m + 1)
                    mm(psB1[:, 2 * P:3 * P], kn[p][:, c, :], pT[:, :], start=c == 0).then_inc(S.o_ps, 1)

                def c_wo(b):
                    n, h, p = b
                    pe.wait_ge(S.og_ready, NC * (n + 1))
                    for c in range(NC):
                        last = mm(psB0[:, c * P:(c + 1) * P], og[:, c, :], wo[:, :])
                    last.then_inc(S.y_ps, 1)

                def c_T(b):
                    n, h, p = b
                    pe.wait_ge(S.xn2_ready, NC * (n + 1))
                    for c in range(NC):
                        last = nc.tensor.transpose(psB1[:, c * P:(c + 1) * P], xn2[:, c, :], eye[:, 0, :])
                    last.then_inc(S.xn2T_ps, 1)

                def c_logits(b):
                    n, h, p = b
                    pe.wait_ge(S.xn2T_ready, n + 1)
                    for c in range(NC):
                        last = mm(psB0[:, c * E:(c + 1) * E], xn2T[:, c * P:(c + 1) * P], w_router[:, :])
                    last.then_inc(S.log_ps, 1)

                def c_h(b, k):
                    n, h, p = b
                    if k:
                        pe.wait_ge(S.route, 12 * n + 1)
                    mm((psB0 if k else psB1)[:, :], w_gate[:, k * P:(k + 1) * P], xn2T[:, :]).then_inc(S.h_ps, 1)

                def c_cum(b):
                    n, h, p = b
                    pe.wait_ge(S.mask_ready, 9 * (n + 1))
                    pe.wait_ge(S.h_ready, KH * n + 1)
                    m16, b16 = [t[:, :, :].rearrange("p c e -> p (c e)") for t in (mask16, before16)]
                    mm(psB1[:, 0:NC * E], prefix16[:, 0, :], m16, stop=False)
                    mm(psB1[:, 0:NC * E], prefix16[:, 1, :], b16, start=False).then_inc(S.cum_ps, 1)

                def f_mm(b, c, half):
                    n, h, p = b
                    if c == 0 and half == 0:
                        pe.wait_ge(S.h_ready, KH * (n + 1))
                    if c == 0:
                        wait(pe, S.f_acc, NC * E * n - 4 * (1 - half))
                    else:
                        pe.wait_ge(S.f_acc, NC * E * n + E * (c - 1) + 4 * (half + 1))
                    for k in range(KH):
                        last = mm(psF[half][:, :], hT[p][:, k, c * P:(c + 1) * P],
                                  w_down[:, k, 4 * half:4 * half + 4, :].rearrange("p e d -> p (e d)"),
                                  start=k == 0, stop=k == KH - 1)
                    last.then_inc(S.f_ps, 1)

                if b1: a_Z(b1, 3)
                if b2: c_wo(b2)
                if b0: a_T(b0)
                if b1: a_R(b1, 4)
                if b0: a_alpha(b0); a_kv(b0, 0)
                if b1: a_Z(b1, 4)
                if b0: a_kv(b0, 1); a_kv(b0, 2)
                if b1: a_R(b1, 5)
                if b2: c_T(b2)
                if b1: a_Z(b1, 5)
                if b0: a_kv(b0, 3)
                if b2: c_logits(b2); c_h(b2, 0)
                if b1: a_X64(b1)
                if b2: c_h(b2, 1)
                if b1: a_R(b1, 6)
                if b2: c_cum(b2)
                if b1: a_Z(b1, 6)
                if b0: a_g(b0)
                if b1: b_w(b1, 0)
                if b2: f_mm(b2, 0, 0)
                if b1: b_qw_s(b1, 0)
                if b2: f_mm(b2, 0, 1)
                if b1: b_o(b1, 0)
                if b0: a_kT(b0)
                if b1: b_rhs(b1, 1)
                if b2: f_mm(b2, 1, 0)
                if b0: a_kk(b0)
                if b1: b_w(b1, 1)
                if b2: f_mm(b2, 1, 1)
                if b1: b_qw_s(b1, 1)
                if b0: a_R(b0, 0)
                if b2: f_mm(b2, 2, 0)
                if b1: b_o(b1, 1); b_rhs(b1, 2)
                if b2: f_mm(b2, 2, 1)
                if b0: a_R(b0, 1)
                if b1: b_w(b1, 2)
                if b2: f_mm(b2, 3, 0)
                if b0: a_Z(b0, 1)
                if b1: b_qw_s(b1, 2)
                if b2: f_mm(b2, 3, 1)
                if b0: a_R(b0, 2)
                if b1: b_o(b1, 2); b_rhs(b1, 3)
                if b0: a_q(b0)
                if b1: b_w(b1, 3)
                if b0: a_Z(b0, 2)
                if b1: b_qw_s(b1, 3)
                if b0: a_R(b0, 3)
                if b1: b_o(b1, 3)

            batches(pe, iteration)


_INS = ["L0_attn_x", "L0_attn_Wq", "L0_attn_bq", "L0_attn_Wk", "L0_attn_bk", "L0_attn_Wv", "L0_attn_bv", "L0_attn_Wa",
        "L0_attn_ba", "L0_attn_Wb", "L0_attn_bb", "L0_attn_Wg", "L0_attn_bg", "L0_attn_Wo", "L0_attn_bo",
        "L0_ffn_w_router", "L0_ffn_w_gate", "L0_ffn_w_down"]


def kernel(**inputs):
    import numpy as np
    import concourse.bacc as bacc
    from concourse.bass_utils import run_bass_kernel_spmd

    nc = bacc.Bacc("TRN2", target_bir_lowering=False, num_devices=1)
    arrays = {}

    def dram(name, a):
        a = np.ascontiguousarray(a)
        arrays[f"in_{name}"] = a
        return nc.dram_tensor(f"in_{name}", a.shape, mybir.dt.from_np(a.dtype), kind="ExternalInput").ap()

    ins = {n: dram(n, inputs[n]) for n in _INS}
    ins["w_router_T"] = dram("w_router_T", np.transpose(np.asarray(inputs["L0_ffn_w_router"])))
    ins["w_gate_T"] = dram("w_gate_T", np.transpose(np.asarray(inputs["L0_ffn_w_gate"])))
    ins["w_down_T"] = dram("w_down_T", np.transpose(np.asarray(inputs["L0_ffn_w_down"]), (2, 0, 1)))
    nb, nt, _ = inputs["L0_attn_x"].shape
    chunks, experts = nt // P, inputs["L0_ffn_w_router"].shape[0]
    r, c = np.arange(P)[:, None], np.arange(P)[None, :]
    cq = np.arange(Q)[None, :]
    pair = [(r % Q // m % 2 == 0) & (cq // m == r % Q // m + 1) for m in SMALL]
    f = np.float32
    consts = {
        "eye": dram("eye", np.stack([np.eye(P, dtype=f)] * chunks, 1)),
        "eye_c": dram("eye_c", np.stack([(r % Q == cq).astype(f)] * chunks, 1)),
        "pair_mask": dram("pair_mask", -np.stack([m.astype(f) for m in pair], 1)),
        "prefix": dram("prefix", np.stack([(r <= c).astype(f), np.ones((P, P), f)], 1)),
        "prio": dram("prio", np.broadcast_to(np.arange(experts, 0, -1, dtype=f), (P, chunks, experts))),
    }
    out = nc.dram_tensor("out_y", inputs["L0_attn_x"].shape, F32, kind="ExternalOutput").ap()
    gated_delta_moe_kernel(nc, ins, consts, out)
    return run_bass_kernel_spmd(nc, [arrays], core_ids=[0]).results[0]["out_y"]
```

```python
from contextlib import ExitStack

import concourse.bass as bass
from concourse import mybir

F32 = mybir.dt.float32
BF16 = mybir.dt.bfloat16
F32R = mybir.dt.float32r
ALU = mybir.AluOpType
ACT = mybir.ActivationFunctionType
AX = mybir.AxisListType

P = 128
Q = 32
SMALL = (1, 2, 4, 8, 16)


def gated_delta_moe_kernel(nc, ins, consts, out):
    x = ins["L0_attn_x"]
    B, T, D = x.shape
    NC = T // P
    E = ins["L0_ffn_w_router"].shape[0]
    HID = ins["L0_ffn_w_gate"].shape[0]
    KH = HID // P
    CAPACITY = -(-(B * T * 5) // (4 * E))
    KVW = 2 * P + 1
    NS = len(SMALL)
    NR = NS + 2
    QUADS = P // Q
    assert D == P and T % P == 0 and B % 2 == 0 and B >= 4 and E == 8

    with ExitStack() as ctx:
        def sb(name, shape, dt=F32):
            return ctx.enter_context(nc.sbuf_tensor(name, shape, dt))

        def bank(name):
            return ctx.enter_context(nc.psum_tensor(name, [P, 512], F32))

        def sem(name):
            return ctx.enter_context(nc.semaphore(name))

        eye = sb("eye", [P, NC, P])
        eye_c = sb("eye_c", [P, NC, Q])
        pair_mask = sb("pair_mask", [P, NS, Q])
        prio = sb("prio", [P, NC, E])
        prefix = sb("prefix", [P, 2, P])
        prefix16 = sb("prefix16", [P, 2, P], BF16)
        wqg = sb("wqg", [P, 2, P])
        wa_col = sb("wa_col", [P, 1])
        wa_cut = [sb(f"wa_cut{k}", [P, P], F32R) for k in range(2)]
        wqg_cut = [sb(f"wqg_cut{k}", [P, 2, P], F32R) for k in range(2)]
        wkvb_cut = [sb(f"wkvb_cut{k}", [P, KVW + 1], F32R) for k in range(2)]
        wkvb = sb("wkvb", [P, KVW + 1])
        kvb_bias = sb("kvb_bias", [P, KVW])
        wo = sb("wo", [P, P])
        bo_bc = sb("bo_bc", [P, P])
        bqg_col = sb("bqg_col", [P, 2])
        ba_col = sb("ba_col", [P, 1])
        w_router = sb("w_router", [P, E])
        w_gate = sb("w_gate", [P, HID])
        w_down = sb("w_down", [P, KH, E, P])
        w_down_hi = sb("w_down_hi", [P, KH, E, P], F32R)
        w_down_lo = sb("w_down_lo", [P, KH, E, P], F32R)
        pad = sb("pad", [P, 4])
        neg_half = sb("neg_half", [P, NC])

        xin = [sb(f"xin{p}", [P, NC, P]) for p in range(2)]
        a_st = sb("a_st", [P, NC, 6])
        a_mv = sb("a_mv", [P, NC, 2])
        a_veps = sb("a_veps", [P, NC])
        a_rstd = sb("a_rstd", [P, NC])
        xn = sb("xn", [P, NC, P])
        xnT_cut = [sb(f"xnT_cut{k}", [P, T], F32R) for k in range(2)]
        alpha = sb("alpha", [P, NC, P])
        alpha0 = sb("alpha0", [P, T + 8])
        alpha_first = sb("alpha_first", [P, T])
        decay_row = [sb(f"decay_row{p}", [P, T]) for p in range(2)]
        gam = sb("gam", [P, T])
        gamT = [sb(f"gamT{p}", [P, T]) for p in range(2)]
        kvb = sb("kvb", [P, NC, KVW + 3])
        ksq = sb("ksq", [P, NC, P])
        kss = sb("kss", [P, NC])
        kss_c = sb("kss_c", [P, NC])
        krn = sb("krn", [P, NC])
        beta = sb("beta", [P, NC])
        decay_col = sb("decay_col", [P, NC])
        neg_ba = [sb(f"neg_ba{p}", [P, NC]) for p in range(2)]
        kn = [sb(f"kn{p}", [P, NC, P]) for p in range(2)]
        kg = [sb(f"kg{p}", [P, NC, P]) for p in range(2)]
        bv = [sb(f"bv{p}", [P, NC, P]) for p in range(2)]
        kT = [sb(f"kT{p}", [P, T]) for p in range(2)]
        qT = [sb(f"qT{p}", [P, T]) for p in range(2)]
        qaT = [sb(f"qaT{p}", [P, T]) for p in range(2)]
        gT = [sb(f"gT{p}", [P, T]) for p in range(2)]
        Lbd = sb("Lbd", [P, NC, P])
        L32 = sb("L32", [P, NC, P])
        L64 = sb("L64", [P, NC, P])
        gamb = sb("gamb", [P, NC, P])
        Zc = sb("Zc", [P, NC, Q])
        Xc = sb("Xc", [P, NC, Q])
        Rc = sb("Rc", [P, NC, Q])
        R64 = sb("R64", [P, NC, 2 * Q])
        Xf = sb("Xf", [P, NC, P])
        X64 = sb("X64", [P, NC, P])
        Zf = [sb(f"Zf{p}", [P, NC, P]) for p in range(2)]

        state = [sb(f"state{p}", [P, 2, P]) for p in range(2)]
        rhs = sb("rhs", [P, P])
        w_wT = sb("w_wT", [P, 2, P])
        pT = sb("pT", [P, P])
        og = sb("og", [P, NC, P])
        x1 = [sb(f"x1_{p}", [P, NC, P]) for p in range(2)]
        c_st = sb("c_st", [P, NC, 6])
        c_mv = sb("c_mv", [P, NC, 2])
        c_veps = sb("c_veps", [P, NC])
        c_rstd = sb("c_rstd", [P, NC])
        xn2 = sb("xn2", [P, NC, P])
        xn2T = sb("xn2T", [P, T])
        sig_h = sb("sig_h", [P, KH, T])
        hT = sb("hT", [P, KH, T])
        hT_hi = [sb(f"hT_hi{p}", [P, KH, T], F32R) for p in range(2)]
        hT_lo = [sb(f"hT_lo{p}", [P, KH, T], F32R) for p in range(2)]
        lg = sb("lg", [P, NC, E])
        top = sb("top", [P, 4, NC])
        rt = [sb(f"rt{n}", [P, NC, E]) for n in range(10)]
        mask16 = sb("mask16", [P, NC, E], BF16)
        before = sb("before", [P, NC + 1, E])
        before16 = sb("before16", [P, NC, E], BF16)
        sums = sb("sums", [P, 4, NC])
        comb = [sb(f"comb{p}", [P, NC, E]) for p in range(2)]
        gated = [sb(f"gated{p}", [P, E, P]) for p in range(2)]
        pair_sum = sb("pair_sum", [P, P])

        psA, psK, psR, psZ, psB0, psB1 = [bank(n) for n in ("psA", "psK", "psR", "psZ", "psB0", "psB1")]
        psF = [bank("psF0"), bank("psF1")]

        names = """early_loaded late_loaded pool_consts act_consts dve_consts proj_cut
            a_stats a_aggr a_veps_ready a_rstd_ready xn_ready
            xnT_ps xnT_ready xnT_lo_ready alpha_ps alpha_ready kv_ps kv_ready kss_ready kssc_ready krn_ready beta_ready
            alpha0_ready gam_ready decay_ready dcol_ready kn_ready kg_ready bv_ready negba_ready
            kT_ps kT_ready q_ps q_ready qa_ready g_ps g_ready kk_ps L_ready gamb_ready R_ps R_ready Z_ps
            Zc_ready Xc_ready X_ready X64_ps X64_ready Zd_ready Zo_ready
            rhs_ps rhs_ready w_ps w_ready qw_ps p_ready s_ps s_ready o_ps og_ready
            y_ps res_ready x1_ready c_stats c_aggr c_veps_ready c_rstd_ready xn2_ready xn2T_ps xn2T_ready
            log_ps log_ready h_ps sigh_ready h_ready route soft mask_ready cum_ps sig_ready comb_ready
            hi_ready lo_ready w_hi_ready w_lo_ready f_ps f_scaled f_pairs f_half f_acc""".split()
        s = {n: sem(n) for n in names}
        S = type("Sems", (), s)
        x_loaded = [sem(f"x_loaded{p}") for p in range(2)]
        res_loaded = [sem(f"res_loaded{p}") for p in range(2)]
        y_stored = [sem(f"y_stored{p}") for p in range(2)]

        block = ctx.enter_context(nc.Block())

        def wait(eng, sm, n):
            if not (isinstance(n, int) and n <= 0):
                eng.wait_ge(sm, n)

        LEAD = 4

        def batches(eng, iteration, depth=3):
            def step(i):
                iteration(*[(n, n // 2, n % 2) if 0 <= n < B else None for n in range(i, i - depth, -1)])

            for i in range(LEAD):
                step(i)
            with eng.Fori(0, (B - LEAD) // 2) as j:
                for k in range(2):
                    iteration(*[(2 * j + (m := LEAD + k - lag), j + m // 2, m % 2) for lag in range(depth)])
            for i in range(B, B + depth - 1):
                step(i)

        def ch(t, c):
            return t[:, c * P:(c + 1) * P]

        def flat(t):
            return t[:, :, :].rearrange("p c d -> p (c d)")

        N_EARLY, N_LATE = 9, 7
        EARLY, LATE = 16 * N_EARLY, 16 * N_LATE

        def first(n):
            return isinstance(n, int) and n == 0

        @block.sync
        def _(sp):
            early = [
                (wkvb[:, :], ins["w_kvb"]), (wqg[:, :, :], ins["w_qg"]), (eye[:, :, :], consts["eye"]),
                (wa_col[:, :], ins["L0_attn_Wa"]), (ba_col[:, :], ins["L0_attn_ba"].partition_broadcast(P)),
                (kvb_bias[:, :], ins["b_kvb"].partition_broadcast(P)), (bqg_col[:, :], ins["b_qg"]),
                (eye_c[:, :, :], consts["eye_c"]), (pair_mask[:, :, :], consts["pair_mask"]),
            ]
            late = [
                (bo_bc[:, :], ins["L0_attn_bo"].partition_broadcast(P)), (wo[:, :], ins["L0_attn_Wo"]),
                (prefix[:, :, :], consts["prefix"]), (w_router[:, :], ins["w_router_T"]),
                (w_gate[:, :], ins["w_gate_T"]), (prio[:, :, :], consts["prio"]),
                (w_down[:, :, :, :], ins["w_down_T"].rearrange("(k p) e d -> p k e d", p=P)),
            ]
            assert (len(early), len(late)) == (N_EARLY, N_LATE)
            sp.dma_start(xin[0][:, :, :], x[0].rearrange("(c p) d -> p c d", p=P)).then_inc(x_loaded[0], 16)
            for dst, src in early:
                sp.dma_start(dst, src).then_inc(S.early_loaded, 16)
            for dst, src in late:
                sp.dma_start(dst, src).then_inc(S.late_loaded, 16)

            def iteration(b0, b1, b2, b3):
                def load(b):
                    n, h, p = b
                    if first(n):
                        return
                    wait(sp, S.xn_ready, NC * (n - 1))
                    sp.dma_start(xin[p][:, :, :], x[n].rearrange("(c p) d -> p c d", p=P)).then_inc(x_loaded[p], 16)

                def load_residual(b):
                    n, h, p = b
                    wait(sp, y_stored[p], 16 * h)
                    sp.dma_start(x1[p][:, :, :], x[n].rearrange("(c p) d -> p c d", p=P)).then_inc(res_loaded[p], 16)

                def store(b):
                    n, h, p = b
                    sp.wait_ge(S.f_acc, NC * (n + 1))
                    sp.dma_start(out[n].rearrange("(c p) d -> p c d", p=P), x1[p][:, :, :]).then_inc(y_stored[p], 16)

                if b0: load(b0)
                if b3: store(b3)
                if b1: load_residual(b1)

            batches(sp, iteration, 4)
            for p in range(2):
                sp.wait_ge(y_stored[p], 16 * (B // 2))

        @block.gpsimd
        def _(pool):
            pool.memset(neg_half[:, :], -0.5).then_inc(S.pool_consts, 1)
            pool.wait_ge(S.pool_consts, 1)

            def cut_projections():
                pool.wait_ge(S.act_consts, 3)
                for cut, w in ((wa_cut, wa_col[:, :].to_broadcast([P, P])), (wkvb_cut, wkvb[:, :]), (wqg_cut, wqg[:, :, :])):
                    hi, lo = [t[:, :, :] if len(t.shape) == 3 else t[:, :] for t in cut]
                    pool.tensor_tensor(lo, w, hi.bitcast(F32), ALU.subtract).then_inc(S.proj_cut, 1)

            def iteration(b0, b1, b2):
                def a_rstd_pow(b):
                    n, h, p = b
                    pool.wait_ge(S.a_veps_ready, n + 1)
                    pool.tensor_tensor(a_rstd[:, :], a_veps[:, :], neg_half[:, :], ALU.pow).then_inc(S.a_rstd_ready, 1)
                    if first(n):
                        cut_projections()

                def a_krn(b):
                    n, h, p = b
                    pool.wait_ge(S.kssc_ready, n + 1)
                    pool.tensor_tensor(krn[:, :], kss_c[:, :], neg_half[:, :], ALU.pow).then_inc(S.krn_ready, 1)

                def a_qa(b):
                    n, h, p = b
                    pool.wait_ge(S.q_ready, n + 1)
                    pool.wait_ge(S.decay_ready, n + 1)
                    wait(pool, S.og_ready, NC * (n - 1))
                    pool.tensor_tensor(qaT[p][:, :], qT[p][:, :], decay_row[p][:, :], ALU.mult).then_inc(S.qa_ready, 1)

                def c_bias(b):
                    n, h, p = b
                    if first(n):
                        pool.wait_ge(S.late_loaded, LATE)
                        pool.wait_ge(S.w_hi_ready, 1)
                        pool.tensor_tensor(w_down_lo[:, :, :, :], w_down[:, :, :, :],
                                           w_down_hi[:, :, :, :].bitcast(F32), ALU.subtract).then_inc(S.w_lo_ready, 1)
                    pool.wait_ge(res_loaded[p], 16 * (h + 1))
                    pool.tensor_tensor(x1[p][:, :, :], x1[p][:, :, :],
                                       bo_bc[:, :].unsqueeze(1).to_broadcast([P, NC, P]), ALU.add).then_inc(S.res_ready, 1)

                def h_lo(b, k):
                    n, h, p = b
                    pool.wait_ge(S.hi_ready, KH * n + k + 1)
                    wait(pool, S.f_scaled, NC * E * (n - 1))
                    pool.tensor_tensor(hT_lo[p][:, k, :], hT[:, k, :], hT_hi[p][:, k, :].bitcast(F32),
                                       ALU.subtract).then_inc(S.lo_ready, 1)

                def f_add(b, c):
                    n, h, p = b
                    g = NC * n + c
                    pool.wait_ge(S.f_scaled, E * (g + 1))
                    rows = gated[c % 2]
                    pool.tensor_tensor(rows[:, 0:4, :], rows[:, 0:4, :], rows[:, 4:8, :], ALU.add).then_inc(S.f_pairs, 1)
                    pool.wait_ge(S.f_pairs, 2 * g + 1)
                    pool.tensor_tensor(rows[:, 0:2, :], rows[:, 0:2, :], rows[:, 2:4, :], ALU.add).then_inc(S.f_pairs, 1)

                def c_rstd_pow(b):
                    n, h, p = b
                    pool.wait_ge(S.c_veps_ready, n + 1)
                    pool.tensor_tensor(c_rstd[:, :], c_veps[:, :], neg_half[:, :], ALU.pow).then_inc(S.c_rstd_ready, 1)

                if b0: a_rstd_pow(b0)
                if b1: c_bias(b1); a_qa(b1)
                if b2: c_rstd_pow(b2)
                if b0: a_krn(b0)
                if b2: h_lo(b2, 0); h_lo(b2, 1); f_add(b2, 0); f_add(b2, 1); f_add(b2, 2); f_add(b2, 3)

            batches(pool, iteration)

        @block.scalar
        def _(act):
            act.wait_ge(S.early_loaded, EARLY)
            act.wait_ge(S.dve_consts, 9)
            act.activation(wa_cut[0][:, :], wa_col[:, :].to_broadcast([P, P]), ACT.Copy).then_inc(S.act_consts, 1)
            act.activation(wkvb_cut[0][:, :], wkvb[:, :], ACT.Copy).then_inc(S.act_consts, 1)
            act.activation(wqg_cut[0][:, :, :], wqg[:, :, :], ACT.Copy).then_inc(S.act_consts, 1)

            def iteration(b0, b1, b2):
                def w_copy(b, c):
                    n, h, p = b
                    m = NC * n + c
                    act.wait_ge(S.w_ps, m + 1)
                    wait(act, S.og_ready, m)
                    act.activation(w_wT[:, :, :], psB0[:, P:3 * P].rearrange("p (a d) -> p a d", a=2), ACT.Copy).then_inc(S.w_ready, 1)

                def expand_x(b, l):
                    n, h, p = b
                    act.wait_ge(S.Xc_ready, NS * n + l + 1)
                    wait(act, S.Z_ps, (NR - 1) * n + l)
                    for g in range(QUADS):
                        rows = slice(g * Q, g * Q + Q)
                        act.activation(Xf[rows, :, rows], Xc[rows, :, :], ACT.Copy).then_inc(S.X_ready, 1)

                def scaled(dst, src, by, done):
                    for c in range(NC):
                        act.activation(dst[:, c, :], src(c), ACT.Copy, scale=by(c)).then_inc(done, 1)

                def z_diag(b):
                    n, h, p = b
                    act.wait_ge(S.Zc_ready, NS * (n + 1))
                    wait(act, S.w_ps, NC * (n - 1))
                    for g in range(QUADS):
                        rows = slice(g * Q, g * Q + Q)
                        act.activation(Zf[p][rows, :, rows], Zc[rows, :, :], ACT.Copy).then_inc(S.Zd_ready, 1)

                def r_big(b, l, dst, w):
                    n, h, p = b
                    act.wait_ge(S.R_ps, NR * n + l + 1)
                    act.activation(dst[:, :, :], psR[:, 0:NC * w].rearrange("p (c t) -> p c t", c=NC), ACT.Copy,
                                   scale=-1.0).then_inc(S.R_ready, 1)

                def z_off32(b):
                    n, h, p = b
                    act.wait_ge(S.Z_ps, (NR - 1) * n + NS)
                    for g in (0, 2):
                        act.activation(Zf[p][g * Q:g * Q + Q, :, g * Q + Q:g * Q + 2 * Q],
                                       psZ[g * Q:g * Q + Q, 0:NC * Q].rearrange("p (c t) -> p c t", c=NC),
                                       ACT.Copy).then_inc(S.Zo_ready, 1)

                def x64(b):
                    n, h, p = b
                    act.wait_ge(S.X64_ps, n + 1)
                    act.activation(flat(X64), psZ[:, :], ACT.Copy).then_inc(S.X64_ready, 1)

                def z_off64(b):
                    n, h, p = b
                    act.wait_ge(S.Z_ps, (NR - 1) * (n + 1))
                    act.activation(Zf[p][0:2 * Q, :, 2 * Q:P],
                                   psZ[0:2 * Q, 0:NC * 2 * Q].rearrange("p (c t) -> p c t", c=NC),
                                   ACT.Copy).then_inc(S.Zo_ready, 1)

                def a_xnT(b):
                    n, h, p = b
                    act.wait_ge(S.xnT_ps, n + 1)
                    act.activation(xnT_cut[0][:, :], psA[:, :], ACT.Copy).then_inc(S.xnT_ready, 1)

                def a_alpha(b):
                    n, h, p = b
                    act.wait_ge(S.alpha_ps, n + 1)
                    wait(act, S.dcol_ready, n)
                    act.activation(flat(alpha), psK[:, :], ACT.Sigmoid, bias=ba_col[:, 0:1]).then_inc(S.alpha_ready, 1)

                def a_kss(b):
                    n, h, p = b
                    for c in range(NC):
                        act.wait_ge(S.kv_ready, NC * n + c + 1)
                        act.activation(ksq[:, c, :], kvb[:, c, 0:P], ACT.Square, accum_out=kss[:, c:c + 1]).then_inc(S.kss_ready, 1)
                    wait(act, S.negba_ready, n)
                    act.activation(beta[:, :], kvb[:, :, 2 * P], ACT.Sigmoid).then_inc(S.beta_ready, 1)

                def a_gamb(b):
                    n, h, p = b
                    act.wait_ge(S.beta_ready, n + 1)
                    act.wait_ge(S.gam_ready, 2 * n + 1)
                    wait(act, S.L_ready, 7 * n)
                    scaled(gamb, lambda c: ch(gam, c), lambda c: beta[:, c:c + 1], S.gamb_ready)

                def a_kT(b):
                    n, h, p = b
                    act.wait_ge(S.kT_ps, n + 1)
                    wait(act, S.w_ps, NC * (n - 1))
                    act.activation(kT[p][:, :], psA[:, :], ACT.Copy).then_inc(S.kT_ready, 1)

                def a_q(b):
                    n, h, p = b
                    act.wait_ge(S.q_ps, n + 1)
                    act.activation(qT[p][:, :], psA[:, :], ACT.Identity, bias=bqg_col[:, 0:1]).then_inc(S.q_ready, 1)

                def a_g(b):
                    n, h, p = b
                    act.wait_ge(S.g_ps, n + 1)
                    act.activation(gT[p][:, :], psK[:, :], ACT.Sigmoid, bias=bqg_col[:, 1:2]).then_inc(S.g_ready, 1)

                def a_bv(b):
                    n, h, p = b
                    if first(n):
                        act.wait_ge(S.late_loaded, LATE)
                        act.activation(prefix16[:, :, :], prefix[:, :, :], ACT.Copy).then_inc(S.act_consts, 1)
                        act.activation(w_down_hi[:, :, :, :], w_down[:, :, :, :], ACT.Copy).then_inc(S.w_hi_ready, 1)
                    act.wait_ge(S.beta_ready, n + 1)
                    scaled(bv[p], lambda c: kvb[:, c, P:2 * P], lambda c: beta[:, c:c + 1], S.bv_ready)

                def a_kg(b):
                    n, h, p = b
                    act.wait_ge(S.kn_ready, n + 1)
                    act.wait_ge(S.gam_ready, 2 * (n + 1))
                    scaled(kg[p], lambda c: kn[p][:, c, :], lambda c: gamT[p][:, c * P + P - 1:c * P + P], S.kg_ready)

                def c_xnT(b):
                    n, h, p = b
                    act.wait_ge(S.xn2T_ps, n + 1)
                    act.activation(xn2T[:, :], psB1[:, :], ACT.Copy).then_inc(S.xn2T_ready, 1)

                def c_sigh(b, k):
                    n, h, p = b
                    act.wait_ge(S.h_ps, KH * n + k + 1)
                    wait(act, S.h_ready, KH * (n - 1) + k + 1)
                    act.activation(sig_h[:, k, :], (psB0 if k else psB1)[:, :], ACT.Sigmoid).then_inc(S.sigh_ready, 1)

                def h_hi(b, k):
                    n, h, p = b
                    act.wait_ge(S.h_ready, KH * n + k + 1)
                    wait(act, S.f_scaled, NC * E * (n - 1))
                    act.activation(hT_hi[p][:, k, :], hT[:, k, :], ACT.Copy).then_inc(S.hi_ready, 1)

                def f_gate(b, c, half):
                    n, h, p = b
                    g = NC * n + c
                    act.wait_ge(S.f_ps, 2 * g + half + 1)
                    if c == 0 and half == 0:
                        act.wait_ge(S.comb_ready, 9 * (n + 1))
                    wait(act, S.f_half, g - 1)
                    for e in range(4):
                        act.activation(gated[c % 2][:, 4 * half + e, :], psF[half][:, e * P:(e + 1) * P], ACT.Copy,
                                       scale=comb[p][:, c, 4 * half + e:4 * half + e + 1]).then_inc(S.f_scaled, 1)

                def c_soft(b):
                    n, h, p = b
                    act.wait_ge(S.soft, 2 * n + 1)
                    act.activation(rt[6][:, :, :], rt[5][:, :, :], ACT.Sigmoid).then_inc(S.sig_ready, 1)
                    act.activation(rt[7][:, :, :], rt[5][:, :, :], ACT.Sigmoid, scale=-1.0).then_inc(S.sig_ready, 1)

                if b0: a_xnT(b0)
                if b1: z_diag(b1)
                if b0: a_alpha(b0)
                if b1: expand_x(b1, 4); r_big(b1, NS, Rc, Q); z_off32(b1)
                if b2: c_xnT(b2)
                if b0: a_kss(b0)
                if b2: c_sigh(b2, 0)
                if b0: a_gamb(b0)
                if b1: x64(b1)
                if b2: h_hi(b2, 0); c_sigh(b2, 1)
                if b1: r_big(b1, NS + 1, R64, 2 * Q)
                if b0: a_kT(b0)
                if b2: h_hi(b2, 1); c_soft(b2)
                if b0: a_kg(b0)
                if b1: z_off64(b1)
                if b2: f_gate(b2, 0, 0); f_gate(b2, 0, 1)
                if b1: w_copy(b1, 0)
                if b2: f_gate(b2, 1, 0); f_gate(b2, 1, 1); f_gate(b2, 2, 0); f_gate(b2, 2, 1)
                if b0: expand_x(b0, 0)
                if b1: w_copy(b1, 1)
                if b2: f_gate(b2, 3, 0); f_gate(b2, 3, 1)
                if b0: a_q(b0); expand_x(b0, 1)
                if b1: w_copy(b1, 2)
                if b0: a_g(b0); expand_x(b0, 2); a_bv(b0)
                if b1: w_copy(b1, 3)
                if b0: expand_x(b0, 3)

            batches(act, iteration)

        @block.vector
        def _(dve):
            dve.memset(alpha0[:, :], 0.0).then_inc(S.dve_consts, 1)
            dve.memset(alpha_first[:, :], 0.0).then_inc(S.dve_consts, 1)
            dve.memset(before[:, :, :], 0.0).then_inc(S.dve_consts, 1)
            for t in (Lbd, L32, L64, Xf, *Zf):
                dve.memset(t[:, :, :], 0.0).then_inc(S.dve_consts, 1)
            dve.wait_ge(S.dve_consts, 9)

            def iteration(b0, b1, b2):
                def a_norm(b):
                    n, h, p = b
                    dve.wait_ge(x_loaded[p], 16 * (h + 1))
                    for c in range(NC):
                        dve.bn_stats(a_st[:, c, :], xin[p][:, c, :]).then_inc(S.a_stats, 1)
                    dve.wait_ge(S.a_stats, NC * (n + 1))
                    dve.memset(pad[:, 0:1], 0.0)
                    for c in range(NC):
                        dve.bn_aggr(a_mv[:, c, :], a_st[:, c, :]).then_inc(S.a_aggr, 1)
                    dve.wait_ge(S.a_aggr, NC * (n + 1))
                    dve.tensor_scalar(a_veps[:, :], a_mv[:, :, 1], 1e-5, None, ALU.add).then_inc(S.a_veps_ready, 1)

                def a_xn(b):
                    n, h, p = b
                    dve.wait_ge(S.a_rstd_ready, n + 1)
                    for c in range(NC):
                        dve.tensor_scalar(xn[:, c, :], xin[p][:, c, :], a_mv[:, c, 0:1], a_rstd[:, c:c + 1],
                                          ALU.subtract, ALU.mult).then_inc(S.xn_ready, 1)

                def a_xnT_lo(b):
                    n, h, p = b
                    dve.wait_ge(S.xnT_ready, n + 1)
                    dve.tensor_tensor(xnT_cut[1][:, :], psA[:, :], xnT_cut[0][:, :].bitcast(F32),
                                      ALU.subtract).then_inc(S.xnT_lo_ready, 1)

                def a_kv(b, c):
                    n, h, p = b
                    if first(n) and c == 0:
                        dve.wait_ge(S.early_loaded, EARLY)
                    dve.wait_ge(S.kv_ps, NC * n + c + 1)
                    dve.tensor_tensor(kvb[:, c, 0:KVW], (psK if c % 2 else psA)[:, 0:KVW], kvb_bias[:, :], ALU.add).then_inc(S.kv_ready, 1)

                def a_decay(b):
                    n, h, p = b
                    dve.wait_ge(S.alpha_ready, n + 1)
                    dve.tensor_copy(alpha0[:, 0:T].rearrange("p (c t) -> p c t", c=NC)[:, :, 1:P],
                                    alpha[:, :, 1:P]).then_inc(S.alpha0_ready, 1)
                    dve.tensor_copy(alpha_first[:, :].rearrange("p (c t) -> p c t", c=NC)[:, :, 0],
                                    alpha[:, :, 0]).then_inc(S.alpha0_ready, 1)
                    dve.wait_ge(S.alpha0_ready, 2 * (n + 1))
                    wait(dve, S.gamb_ready, NC * n)
                    dve.tensor_tensor_scan(gam[:, ::-1], alpha0[:, 1:T + 1][:, ::-1], flat(eye)[:, ::-1], 0.0,
                                           ALU.mult, ALU.add).then_inc(S.gam_ready, 1)
                    wait(dve, S.og_ready, NC * (n - 1))
                    dve.tensor_tensor_scan(gamT[p][:, :], alpha0[:, 0:T], flat(eye), 0.0,
                                           ALU.mult, ALU.add).then_inc(S.gam_ready, 1)
                    dve.tensor_tensor_scan(decay_row[p][:, :], alpha0[:, 0:T], alpha_first[:, :], 0.0,
                                           ALU.mult, ALU.add).then_inc(S.decay_ready, 1)
                    dve.wait_ge(S.gam_ready, 2 * (n + 1))
                    dve.tensor_tensor(decay_col[:, :], gam[:, :].rearrange("p (c t) -> p c t", c=NC)[:, :, 0],
                                      alpha[:, :, 0], ALU.mult).then_inc(S.dcol_ready, 1)

                def a_knorm(b):
                    n, h, p = b
                    dve.wait_ge(S.kss_ready, NC * (n + 1))
                    dve.tensor_scalar(kss_c[:, :], kss[:, :], 1e-24, None, ALU.max).then_inc(S.kssc_ready, 1)

                def a_negba(b):
                    n, h, p = b
                    dve.wait_ge(S.beta_ready, n + 1)
                    dve.wait_ge(S.dcol_ready, n + 1)
                    wait(dve, S.rhs_ready, (NC - 1) * (n - 1))
                    dve.scalar_tensor_tensor(neg_ba[p][:, :], decay_col[:, :], -1.0, beta[:, :],
                                             ALU.mult, ALU.mult).then_inc(S.negba_ready, 1)

                def a_keys(b):
                    n, h, p = b
                    dve.wait_ge(S.krn_ready, n + 1)
                    dve.tensor_tensor(kn[p][:, :, :], kvb[:, :, 0:P], krn[:, :].unsqueeze(2).to_broadcast([P, NC, P]),
                                      ALU.mult).then_inc(S.kn_ready, 1)

                def a_L(b):
                    n, h, p = b
                    dve.wait_ge(S.kk_ps, n + 1)
                    dve.wait_ge(S.gamb_ready, NC * (n + 1))
                    wait(dve, S.R_ps, NR * n)
                    kk = psR[:, :].rearrange("p (c t) -> p c t", c=NC)
                    parts = [(Lbd, slice(g * Q, g * Q + Q), slice(g * Q, g * Q + Q)) for g in range(QUADS)]
                    parts += [(L32, slice(g * Q, g * Q + Q), slice(g * Q - Q, g * Q)) for g in (1, 3)]
                    parts += [(L64, slice(2 * Q, P), slice(0, 2 * Q))]
                    for dst, rows, cols in parts:
                        dve.tensor_tensor(dst[rows, :, cols], kk[rows, :, cols], gamb[rows, :, cols],
                                          ALU.mult).then_inc(S.L_ready, 1)

                def a_R(b, l):
                    n, h, p = b
                    dve.wait_ge(S.R_ps, NR * n + l + 1)
                    dve.tensor_tensor(Rc[:, :, :], psR[:, 0:NC * Q].rearrange("p (c t) -> p c t", c=NC),
                                      pair_mask[:, l, :].unsqueeze(1).to_broadcast([P, NC, Q]), ALU.mult).then_inc(S.R_ready, 1)

                def a_Z(b, l):
                    n, h, p = b
                    if l == 0:
                        dve.wait_ge(S.R_ready, NR * n + 1)
                        wait(dve, S.Zd_ready, QUADS * n)
                        dve.tensor_tensor(Zc[:, :, :], eye_c[:, :, :], Rc[:, :, :], ALU.add).then_inc(S.Zc_ready, 1)
                    else:
                        dve.wait_ge(S.Z_ps, (NR - 1) * n + l)
                        dve.tensor_tensor(Zc[:, :, :], Zc[:, :, :], psZ[:, 0:NC * Q].rearrange("p (c t) -> p c t", c=NC),
                                          ALU.add).then_inc(S.Zc_ready, 1)
                    dve.wait_ge(S.Zc_ready, NS * n + l + 1)
                    wait(dve, S.X_ready, QUADS * (NS * n + l))
                    dve.transpose(Xc[:, :, :].rearrange("p c t -> p (c t)"),
                                  Zc[:, :, :].rearrange("p c t -> p (c t)")).then_inc(S.Xc_ready, 1)

                def b_rhs(b, c):
                    n, h, p = b
                    dve.wait_ge(S.rhs_ps, (NC - 1) * n + c)
                    dve.scalar_tensor_tensor(rhs[:, :], psB0[:, 0:P], neg_ba[p][:, c:c + 1], bv[p][:, c, :],
                                             ALU.mult, ALU.add).then_inc(S.rhs_ready, 1)

                def b_p(b, c):
                    n, h, p = b
                    dve.wait_ge(S.qw_ps, NC * n + c + 1)
                    dve.tensor_tensor(pT[:, :], psB0[:, 3 * P:4 * P], ch(gamT[p], c), ALU.mult).then_inc(S.p_ready, 1)

                def b_state(b, c):
                    n, h, p = b
                    m = (NC - 1) * n + c
                    dve.wait_ge(S.s_ps, m + 1)
                    both = psB1[:, 0:2 * P].rearrange("p (a d) -> p a d", a=2)
                    if c == 0:
                        dve.tensor_copy(state[1][:, :, :], both).then_inc(S.s_ready, 1)
                    else:
                        dve.wait_ge(S.s_ready, m)
                        dve.scalar_tensor_tensor(state[(c + 1) % 2][:, :, :], state[c % 2][:, :, :],
                                                 decay_row[p][:, c * P + P - 1:c * P + P], both,
                                                 ALU.mult, ALU.add).then_inc(S.s_ready, 1)

                def b_o(b, c):
                    n, h, p = b
                    dve.wait_ge(S.o_ps, NC * n + c + 1)
                    dve.tensor_tensor(og[:, c, :], psB1[:, 2 * P:3 * P], ch(gT[p], c), ALU.mult).then_inc(S.og_ready, 1)

                def c_norm(b):
                    n, h, p = b
                    dve.wait_ge(S.y_ps, n + 1)
                    dve.wait_ge(S.res_ready, n + 1)
                    dve.tensor_tensor(flat(x1[p]), psB0[:, :], flat(x1[p]), ALU.add).then_inc(S.x1_ready, 1)
                    dve.wait_ge(S.x1_ready, n + 1)
                    for c in range(NC):
                        dve.bn_stats(c_st[:, c, :], x1[p][:, c, :]).then_inc(S.c_stats, 1)
                    dve.wait_ge(S.c_stats, NC * (n + 1))
                    dve.memset(pad[:, 1:2], 0.0)
                    for c in range(NC):
                        dve.bn_aggr(c_mv[:, c, :], c_st[:, c, :]).then_inc(S.c_aggr, 1)
                    dve.wait_ge(S.c_aggr, NC * (n + 1))
                    dve.tensor_scalar(c_veps[:, :], c_mv[:, :, 1], 1e-5, None, ALU.add).then_inc(S.c_veps_ready, 1)

                def c_xn(b):
                    n, h, p = b
                    dve.wait_ge(S.c_rstd_ready, n + 1)
                    for c in range(NC):
                        dve.tensor_scalar(xn2[:, c, :], x1[p][:, c, :], c_mv[:, c, 0:1], c_rstd[:, c:c + 1],
                                          ALU.subtract, ALU.mult).then_inc(S.xn2_ready, 1)

                def c_h(b, k):
                    n, h, p = b
                    dve.wait_ge(S.sigh_ready, KH * n + k + 1)
                    wait(dve, S.lo_ready, KH * n)
                    dve.tensor_tensor(hT[:, k, :], (psB0 if k else psB1)[:, :], sig_h[:, k, :],
                                      ALU.mult).then_inc(S.h_ready, 1)

                STEPS = 12

                def bc(t):
                    return t.unsqueeze(2).to_broadcast([P, NC, E])

                def c_logits(b):
                    n, h, p = b
                    dve.wait_ge(S.log_ps, n + 1)
                    dve.tensor_copy(lg[:, :, :], psB0[:, 0:NC * E].rearrange("p (c e) -> p c e", c=NC)).then_inc(S.route, 1)

                def c_first(b):
                    n, h, p = b
                    def step(k, ins_):
                        ins_.then_inc(S.route, 1)
                        dve.wait_ge(S.route, STEPS * n + k)
                    if first(n):
                        dve.wait_ge(S.late_loaded, LATE)
                    dve.wait_ge(S.route, STEPS * n + 1)
                    step(2, dve.tensor_reduce(top[:, 0, :], lg[:, :, :], AX.X, ALU.max))
                    dve.tensor_tensor(rt[5][:, :, :], lg[:, :, :], bc(top[:, 0, :]), ALU.subtract).then_inc(S.soft, 1)
                    step(3, dve.tensor_tensor(rt[0][:, :, :], lg[:, :, :], bc(top[:, 0, :]), ALU.is_equal))
                    step(4, dve.tensor_tensor(rt[0][:, :, :], rt[0][:, :, :], prio[:, :, :], ALU.mult))
                    step(5, dve.tensor_reduce(top[:, 1, :], rt[0][:, :, :], AX.X, ALU.max))
                    step(6, dve.tensor_tensor(rt[1][:, :, :], prio[:, :, :], bc(top[:, 1, :]), ALU.is_equal))

                def c_second(b):
                    n, h, p = b
                    def step(k, ins_):
                        ins_.then_inc(S.route, 1)
                        dve.wait_ge(S.route, STEPS * n + k)
                    dve.wait_ge(S.route, STEPS * n + 6)
                    step(7, dve.scalar_tensor_tensor(rt[2][:, :, :], rt[1][:, :, :], -3e38, lg[:, :, :], ALU.mult, ALU.add))
                    step(8, dve.tensor_reduce(top[:, 2, :], rt[2][:, :, :], AX.X, ALU.max))
                    step(9, dve.tensor_tensor(rt[3][:, :, :], rt[2][:, :, :], bc(top[:, 2, :]), ALU.is_equal))
                    step(10, dve.tensor_tensor(rt[3][:, :, :], rt[3][:, :, :], prio[:, :, :], ALU.mult))
                    step(11, dve.tensor_reduce(top[:, 3, :], rt[3][:, :, :], AX.X, ALU.max))
                    step(12, dve.tensor_tensor(rt[4][:, :, :], prio[:, :, :], bc(top[:, 3, :]), ALU.is_equal))

                def c_mask(b):
                    n, h, p = b
                    dve.wait_ge(S.route, STEPS * n + STEPS)
                    dve.tensor_tensor(mask16[:, :, :], rt[4][:, :, :], rt[1][:, :, :], ALU.add).then_inc(S.mask_ready, 1)
                    dve.tensor_tensor(rt[8][:, :, :], rt[4][:, :, :], rt[1][:, :, :], ALU.add).then_inc(S.mask_ready, 1)
                    dve.wait_ge(S.mask_ready, 9 * n + 2)
                    for c in range(NC):
                        dve.tensor_tensor(before[:, c + 1, :], before[:, c, :], rt[8][:, c, :], ALU.add).then_inc(S.mask_ready, 1)
                        dve.wait_ge(S.mask_ready, 9 * n + 3 + c)
                    dve.tensor_copy(before16[:, :, :], before[:, 0:NC, :]).then_inc(S.mask_ready, 1)
                    dve.wait_ge(S.mask_ready, 9 * n + 7)
                    dve.tensor_copy(before[:, 0, :], before[:, NC, :]).then_inc(S.mask_ready, 1)
                    dve.wait_ge(S.mask_ready, 9 * n + 8)
                    dve.memset(sums[:, 0, 0:1], 0.0).then_inc(S.mask_ready, 1)

                CS = 9

                def c_softmax(b):
                    n, h, p = b
                    def step(k, ins_):
                        ins_.then_inc(S.comb_ready, 1)
                        dve.wait_ge(S.comb_ready, CS * n + k)
                    dve.wait_ge(S.sig_ready, 2 * (n + 1))
                    step(1, dve.reciprocal(rt[9][:, :, :], rt[7][:, :, :]))
                    step(2, dve.tensor_tensor(rt[6][:, :, :], rt[6][:, :, :], rt[9][:, :, :], ALU.mult))
                    step(3, dve.tensor_reduce(sums[:, 0, :], rt[6][:, :, :], AX.X, ALU.add))
                    step(4, dve.reciprocal(sums[:, 1, :], sums[:, 0, :]))

                def c_comb(b):
                    n, h, p = b
                    def step(k, ins_):
                        ins_.then_inc(S.comb_ready, 1)
                        dve.wait_ge(S.comb_ready, CS * n + k)
                    dve.wait_ge(S.comb_ready, CS * n + 4)
                    dve.wait_ge(S.cum_ps, n + 1)
                    step(5, dve.scalar_tensor_tensor(rt[2][:, :, :], psB1[:, 0:NC * E].rearrange("p (c e) -> p c e", c=NC),
                                                     float(CAPACITY), rt[8][:, :, :], ALU.is_le, ALU.mult))
                    step(6, dve.tensor_tensor(rt[2][:, :, :], rt[2][:, :, :], rt[6][:, :, :], ALU.mult))
                    step(7, dve.tensor_tensor(rt[2][:, :, :], rt[2][:, :, :], bc(sums[:, 1, :]), ALU.mult))
                    step(8, dve.tensor_reduce(sums[:, 2, :], rt[2][:, :, :], AX.X, ALU.add))
                    dve.tensor_scalar(sums[:, 3, :], sums[:, 2, :], 1e-6, None, ALU.add).then_inc(S.soft, 1)
                    dve.wait_ge(S.soft, 2 * (n + 1))
                    dve.reciprocal(top[:, 0, :], sums[:, 3, :]).then_inc(S.log_ready, 1)
                    dve.wait_ge(S.log_ready, n + 1)
                    wait(dve, S.f_scaled, NC * E * (n - 1))
                    step(9, dve.tensor_tensor(comb[p][:, :, :], rt[2][:, :, :], bc(top[:, 0, :]), ALU.mult))

                def f_add(b, c):
                    n, h, p = b
                    g = NC * n + c
                    dve.wait_ge(S.f_pairs, 2 * (g + 1))
                    wait(dve, S.f_acc, g)
                    dve.tensor_tensor(pair_sum[:, :], gated[c % 2][:, 0, :], gated[c % 2][:, 1, :], ALU.add).then_inc(S.f_half, 1)
                    dve.wait_ge(S.f_half, g + 1)
                    dve.tensor_tensor(x1[p][:, c, :], x1[p][:, c, :], pair_sum[:, :], ALU.add).then_inc(S.f_acc, 1)

                if b0: a_norm(b0)
                if b1: a_Z(b1, 2)
                if b2: b_state(b2, 2); b_p(b2, 2)
                if b1: a_R(b1, 3)
                if b0: a_xn(b0)
                if b2: b_rhs(b2, 3)
                if b1: a_Z(b1, 3)
                if b2: b_o(b2, 2); b_p(b2, 3)
                if b1: a_R(b1, 4)
                if b2: b_o(b2, 3)
                if b0: a_xnT_lo(b0)
                if b1: a_negba(b1); a_Z(b1, 4)
                if b2: c_norm(b2)
                if b0: a_kv(b0, 0); a_kv(b0, 1); a_kv(b0, 2)
                if b2: c_xn(b2)
                if b0: a_kv(b0, 3); a_decay(b0)
                if b2: c_logits(b2)
                if b0: a_knorm(b0)
                if b2: c_first(b2); c_h(b2, 0)
                if b0: a_keys(b0)
                if b2: c_second(b2); c_h(b2, 1); c_mask(b2); c_softmax(b2); c_comb(b2)
                if b0: a_L(b0)
                if b1: b_state(b1, 0)
                if b2: f_add(b2, 0)
                if b1: b_p(b1, 0)
                if b0: a_R(b0, 0); a_Z(b0, 0)
                if b1: b_rhs(b1, 1)
                if b2: f_add(b2, 1)
                if b1: b_o(b1, 0)
                if b2: f_add(b2, 2)
                if b0: a_R(b0, 1)
                if b1: b_state(b1, 1); b_p(b1, 1)
                if b0: a_Z(b0, 1)
                if b1: b_o(b1, 1); b_rhs(b1, 2)
                if b2: f_add(b2, 3)
                if b0: a_R(b0, 2)

            batches(dve, iteration)

        @block.tensor
        def _(pe):
            pe.wait_ge(S.early_loaded, EARLY)
            pe.wait_ge(S.act_consts, 3)
            pe.wait_ge(S.dve_consts, 9)

            def mm(o, lhsT, r, start=True, stop=True):
                return nc.tensor.matmul(o, lhsT, r, start=start, stop=stop)

            def mm_cut(o, lhsT, rhs):
                mm(o, lhsT[0], rhs[0], stop=False)
                mm(o, lhsT[1], rhs[0], start=False, stop=False)
                return mm(o, lhsT[0], rhs[1], start=False)

            def iteration(b0, b1, b2):
                def a_T(b):
                    n, h, p = b
                    wait(pe, S.q_ready, n)
                    for c in range(NC):
                        pe.wait_ge(S.xn_ready, NC * n + c + 1)
                        last = nc.tensor.transpose(psA[:, c * P:(c + 1) * P], xn[:, c, :], eye[:, 0, :])
                    last.then_inc(S.xnT_ps, 1)

                def a_alpha(b):
                    n, h, p = b
                    if first(n):
                        pe.wait_ge(S.proj_cut, 3)
                    pe.wait_ge(S.xnT_lo_ready, n + 1)
                    wait(pe, S.g_ready, n)
                    mm_cut(psK[:, :], [t[:, :] for t in wa_cut], [t[:, :] for t in xnT_cut]).then_inc(S.alpha_ps, 1)

                def a_kv(b, c):
                    n, h, p = b
                    if c == 0:
                        wait(pe, S.kn_ready, n)
                        wait(pe, S.bv_ready, NC * n)
                    elif c == 1:
                        pe.wait_ge(S.alpha_ready, n + 1)
                    else:
                        pe.wait_ge(S.kv_ready, NC * n + c - 1)
                    mm_cut((psK if c % 2 else psA)[:, 0:KVW + 1], [ch(t, c) for t in xnT_cut], [t[:, :] for t in wkvb_cut]).then_inc(S.kv_ps, 1)

                def a_kT(b):
                    n, h, p = b
                    pe.wait_ge(S.kn_ready, n + 1)
                    for c in range(NC):
                        last = nc.tensor.transpose(psA[:, c * P:(c + 1) * P], kn[p][:, c, :], eye[:, 0, :])
                    last.then_inc(S.kT_ps, 1)

                def a_kk(b):
                    n, h, p = b
                    pe.wait_ge(S.kT_ready, n + 1)
                    wait(pe, S.R_ready, NR * n)
                    for c in range(NC):
                        last = mm(psR[:, c * P:(c + 1) * P], ch(kT[p], c), ch(kT[p], c))
                    last.then_inc(S.kk_ps, 1)

                def a_q(b):
                    n, h, p = b
                    pe.wait_ge(S.kT_ready, n + 1)
                    mm_cut(psA[:, :], [t[:, 0, :] for t in wqg_cut], [t[:, :] for t in xnT_cut]).then_inc(S.q_ps, 1)

                def a_g(b):
                    n, h, p = b
                    pe.wait_ge(S.kv_ready, NC * (n + 1))
                    mm_cut(psK[:, :], [t[:, 1, :] for t in wqg_cut], [t[:, :] for t in xnT_cut]).then_inc(S.g_ps, 1)

                def a_R(b, l):
                    n, h, p = b
                    if l == 0:
                        pe.wait_ge(S.L_ready, 7 * (n + 1))
                    elif l <= NS:
                        pe.wait_ge(S.Zc_ready, NS * n + l)
                    else:
                        pe.wait_ge(S.Zo_ready, 3 * n + 2)
                    w = 2 * Q if l > NS else Q
                    for c in range(NC):
                        src = eye_c[:, c, :] if l == 0 else Zc[:, c, :] if l <= NS else Zf[p][:, c, 2 * Q:P]
                        last = mm(psR[:, c * w:(c + 1) * w], (Lbd, L32, L64)[max(0, l - NS + 1)][:, c, :], src)
                    last.then_inc(S.R_ps, 1)

                def a_Z(b, l):
                    n, h, p = b
                    pe.wait_ge(S.R_ready, NR * n + l + 1)
                    if l <= NS:
                        pe.wait_ge(S.X_ready, QUADS * (NS * n + l))
                        if l == 1:
                            wait(pe, S.Zo_ready, 3 * n)
                    else:
                        pe.wait_ge(S.X64_ready, n + 1)
                    w = 2 * Q if l > NS else Q
                    for c in range(NC):
                        last = mm(psZ[:, c * w:(c + 1) * w], (X64 if l > NS else Xf)[:, c, :],
                                  (R64 if l > NS else Rc)[:, c, :])
                    last.then_inc(S.Z_ps, 1)

                def a_X64(b):
                    n, h, p = b
                    pe.wait_ge(S.Zd_ready, QUADS * (n + 1))
                    pe.wait_ge(S.Zo_ready, 3 * n + 2)
                    for c in range(NC):
                        last = nc.tensor.transpose(psZ[:, c * P:(c + 1) * P], Zf[p][:, c, :], eye[:, 0, :])
                    last.then_inc(S.X64_ps, 1)

                def b_rhs(b, c):
                    n, h, p = b
                    pe.wait_ge(S.s_ready, (NC - 1) * n + c)
                    mm(psB0[:, 0:P], ch(kT[p], c), state[c % 2][:, 1, :]).then_inc(S.rhs_ps, 1)

                def b_w(b, c):
                    n, h, p = b
                    if c == 0:
                        pe.wait_ge(S.Zo_ready, 3 * (n + 1))
                        pe.wait_ge(S.bv_ready, NC * (n + 1))
                        wait(pe, S.h_ready, KH * n)
                        wait(pe, S.comb_ready, 9 * n)
                        r = bv[p][:, 0, :]
                    else:
                        pe.wait_ge(S.rhs_ready, (NC - 1) * n + c)
                        r = rhs[:, :]
                    mm(psB0[:, P:2 * P], Zf[p][:, c, :], r)
                    mm(psB0[:, 2 * P:3 * P], r, Zf[p][:, c, :]).then_inc(S.w_ps, 1)

                def b_qw_s(b, c):
                    n, h, p = b
                    m = NC * n + c
                    pe.wait_ge(S.w_ready, m + 1)
                    if c < NC - 1:
                        pe.wait_ge(S.kg_ready, NC * (n + 1))
                        if c:
                            pe.wait_ge(S.og_ready, m)
                        mm(psB1[:, 0:P], w_wT[:, 0, :], kg[p][:, c, :])
                        mm(psB1[:, P:2 * P], kg[p][:, c, :], w_wT[:, 0, :]).then_inc(S.s_ps, 1)
                    pe.wait_ge(S.q_ready, n + 1)
                    mm(psB0[:, 3 * P:4 * P], w_wT[:, 1, :], ch(qT[p], c)).then_inc(S.qw_ps, 1)

                def b_o(b, c):
                    n, h, p = b
                    m = NC * n + c
                    if c < NC - 1:
                        pe.wait_ge(S.s_ready, (NC - 1) * n + c + 1)
                    else:
                        pe.wait_ge(S.og_ready, m)
                    if c > 0:
                        pe.wait_ge(S.qa_ready, n + 1)
                        mm(psB1[:, 2 * P:3 * P], state[c % 2][:, 0, :], ch(qaT[p], c), stop=False)
                    pe.wait_ge(S.p_ready, m + 1)
                    mm(psB1[:, 2 * P:3 * P], kn[p][:, c, :], pT[:, :], start=c == 0).then_inc(S.o_ps, 1)

                def c_wo(b):
                    n, h, p = b
                    if first(n):
                        pe.wait_ge(S.late_loaded, LATE)
                        pe.wait_ge(S.act_consts, 4)
                    pe.wait_ge(S.og_ready, NC * (n + 1))
                    for c in range(NC):
                        last = mm(psB0[:, c * P:(c + 1) * P], og[:, c, :], wo[:, :])
                    last.then_inc(S.y_ps, 1)

                def c_T(b):
                    n, h, p = b
                    pe.wait_ge(S.xn2_ready, NC * (n + 1))
                    for c in range(NC):
                        last = nc.tensor.transpose(psB1[:, c * P:(c + 1) * P], xn2[:, c, :], eye[:, 0, :])
                    last.then_inc(S.xn2T_ps, 1)

                def c_logits(b):
                    n, h, p = b
                    pe.wait_ge(S.xn2T_ready, n + 1)
                    for c in range(NC):
                        last = mm(psB0[:, c * E:(c + 1) * E], xn2T[:, c * P:(c + 1) * P], w_router[:, :])
                    last.then_inc(S.log_ps, 1)

                def c_h(b, k):
                    n, h, p = b
                    if k:
                        pe.wait_ge(S.route, 12 * n + 1)
                    mm((psB0 if k else psB1)[:, :], w_gate[:, k * P:(k + 1) * P], xn2T[:, :]).then_inc(S.h_ps, 1)

                def c_cum(b):
                    n, h, p = b
                    pe.wait_ge(S.mask_ready, 9 * (n + 1))
                    pe.wait_ge(S.h_ready, KH * n + 1)
                    m16, b16 = [t[:, :, :].rearrange("p c e -> p (c e)") for t in (mask16, before16)]
                    mm(psB1[:, 0:NC * E], prefix16[:, 0, :], m16, stop=False)
                    mm(psB1[:, 0:NC * E], prefix16[:, 1, :], b16, start=False).then_inc(S.cum_ps, 1)

                def f_mm(b, c, half):
                    n, h, p = b
                    if c == 0 and half == 0:
                        if first(n):
                            pe.wait_ge(S.w_lo_ready, 1)
                        pe.wait_ge(S.lo_ready, KH * (n + 1))
                    wait(pe, S.f_scaled, 4 * (2 * (NC * n + c) + half - 1))
                    cuts = [(hT_hi, w_down_hi), (hT_lo, w_down_hi), (hT_hi, w_down_lo)]
                    for k in range(KH):
                        for m, (a, w) in enumerate(cuts):
                            last = mm(psF[half][:, :], a[p][:, k, c * P:(c + 1) * P],
                                      w[:, k, 4 * half:4 * half + 4, :].rearrange("p e d -> p (e d)"),
                                      start=k == 0 and m == 0, stop=k == KH - 1 and m == len(cuts) - 1)
                    last.then_inc(S.f_ps, 1)

                if b1: a_Z(b1, 1)
                if b2: b_o(b2, 1); b_rhs(b2, 2)
                if b1: a_R(b1, 2)
                if b2: b_w(b2, 2)
                if b1: a_Z(b1, 2)
                if b2: b_qw_s(b2, 2)
                if b1: a_R(b1, 3)
                if b2: b_o(b2, 2); b_rhs(b2, 3)
                if b1: a_Z(b1, 3)
                if b2: b_w(b2, 3)
                if b1: a_R(b1, 4)
                if b2: b_qw_s(b2, 3)
                if b0: a_T(b0)
                if b2: b_o(b2, 3)
                if b1: a_Z(b1, 4)
                if b2: c_wo(b2)
                if b0: a_alpha(b0)
                if b1: a_R(b1, 5)
                if b0: a_kv(b0, 0); a_kv(b0, 1); a_kv(b0, 2); a_kv(b0, 3)
                if b1: a_Z(b1, 5)
                if b2: c_T(b2)
                if b1: a_X64(b1)
                if b2: c_logits(b2); c_h(b2, 0); c_h(b2, 1)
                if b1: a_R(b1, 6)
                if b0: a_g(b0); a_kT(b0)
                if b1: a_Z(b1, 6)
                if b0: a_kk(b0); a_q(b0)
                if b2: c_cum(b2); f_mm(b2, 0, 0); f_mm(b2, 0, 1)
                if b1: b_w(b1, 0)
                if b2: f_mm(b2, 1, 0); f_mm(b2, 1, 1)
                if b1: b_qw_s(b1, 0)
                if b2: f_mm(b2, 2, 0)
                if b0: a_R(b0, 0)
                if b2: f_mm(b2, 2, 1)
                if b1: b_o(b1, 0); b_rhs(b1, 1)
                if b2: f_mm(b2, 3, 0)
                if b1: b_w(b1, 1)
                if b2: f_mm(b2, 3, 1)
                if b0: a_R(b0, 1)
                if b1: b_qw_s(b1, 1)

            batches(pe, iteration)


_INS = ["L0_attn_x", "L0_attn_Wa", "L0_attn_ba", "L0_attn_Wo", "L0_attn_bo", "L0_ffn_w_router", "L0_ffn_w_gate"]


def kernel(**inputs):
    import numpy as np
    import concourse.bacc as bacc
    from concourse.bass_utils import run_bass_kernel_spmd

    nc = bacc.Bacc("TRN2", target_bir_lowering=False, num_devices=1)
    arrays = {}

    def dram(name, a):
        a = np.ascontiguousarray(a)
        arrays[f"in_{name}"] = a
        return nc.dram_tensor(f"in_{name}", a.shape, mybir.dt.from_np(a.dtype), kind="ExternalInput").ap()

    ins = {n: dram(n, inputs[n]) for n in _INS}
    ins["w_router_T"] = dram("w_router_T", np.transpose(np.asarray(inputs["L0_ffn_w_router"])))
    ins["w_gate_T"] = dram("w_gate_T", np.transpose(np.asarray(inputs["L0_ffn_w_gate"])))
    ins["w_down_T"] = dram("w_down_T", np.transpose(np.asarray(inputs["L0_ffn_w_down"]), (2, 0, 1)))
    attn = {n: np.asarray(inputs[f"L0_attn_{n}"]) for n in ("Wq", "Wk", "Wv", "Wb", "Wg", "bq", "bk", "bv", "bb", "bg")}
    ins["w_qg"] = dram("w_qg", np.stack([attn["Wq"], attn["Wg"]], 1))
    ins["w_kvb"] = dram("w_kvb", np.concatenate([attn["Wk"], attn["Wv"], attn["Wb"], attn["Wb"]], 1))
    ins["b_qg"] = dram("b_qg", np.stack([attn["bq"], attn["bg"]], 1))
    ins["b_kvb"] = dram("b_kvb", np.concatenate([attn["bk"], attn["bv"], attn["bb"]]))
    nb, nt, _ = inputs["L0_attn_x"].shape
    chunks, experts = nt // P, inputs["L0_ffn_w_router"].shape[0]
    r, c = np.arange(P)[:, None], np.arange(P)[None, :]
    cq = np.arange(Q)[None, :]
    pair = [(r % Q // m % 2 == 0) & (cq // m == r % Q // m + 1) for m in SMALL]
    f = np.float32
    consts = {
        "eye": dram("eye", np.stack([np.eye(P, dtype=f)] * chunks, 1)),
        "eye_c": dram("eye_c", np.stack([(r % Q == cq).astype(f)] * chunks, 1)),
        "pair_mask": dram("pair_mask", -np.stack([m.astype(f) for m in pair], 1)),
        "prefix": dram("prefix", np.stack([(r <= c).astype(f), np.ones((P, P), f)], 1)),
        "prio": dram("prio", np.broadcast_to(np.arange(experts, 0, -1, dtype=f), (P, chunks, experts))),
    }
    out = nc.dram_tensor("out_y", inputs["L0_attn_x"].shape, F32, kind="ExternalOutput").ap()
    gated_delta_moe_kernel(nc, ins, consts, out)
    return run_bass_kernel_spmd(nc, [arrays], core_ids=[0]).results[0]["out_y"]
```
